# Optimizing a Trainium2 kernel written in Bass

```python
import numpy as np
import jax
import jax.numpy as jnp

def _softmax(x, axis=-1):
    return jax.nn.softmax(x, axis=axis)

def _gelu(x):
    return jax.nn.gelu(x, approximate=True)

def _silu(x):
    return jax.nn.silu(x)

def _sigmoid(x):
    return jax.nn.sigmoid(x)

def _layernorm(x, axis=-1, eps=1e-05):
    m = jnp.mean(x, axis=axis, keepdims=True)
    v = jnp.var(x, axis=axis, keepdims=True)
    return (x - m) / jnp.sqrt(v + eps)

def _scatter_add(tgt, idx, src, axis=0):
    return tgt.at[idx].add(src)

def _segment_sum(src, seg, n):
    return jax.ops.segment_sum(src, seg, n)
kernel_name = 'mk_adj_resnorm_d4_adj_r2_5505fa'

def setup_inputs(seed: int=0):
    np.random.seed(seed)
    _w = jnp.asarray

    def _rec_inputs():
        import jax
        import jax.numpy as jnp
        _gk = jax.random.key(seed)
        x = -0.0002928 + 1 * jax.random.normal(jax.random.fold_in(_gk, 1), (32, 256, 256), jnp.float32)
        _a = jax.random.bernoulli(jax.random.fold_in(_gk, 2), 0.0625, (32, 256, 256))
        _a = jnp.logical_or(_a, jnp.swapaxes(_a, -1, -2))
        _a = jnp.logical_or(_a, jnp.eye(256, dtype=bool))
        adj = _a
        return (x, adj)
    x, adj = _rec_inputs()

    def _L0_gnn_setup():
        import jax, jax.numpy as jnp
        import numpy as np
        QUERY_DIM = 256
        HEADS = 4
        DIM_HEAD = 64
        INNER = HEADS * DIM_HEAD
        B, N = (4, 1024)
        key = jax.random.key(seed)
        ks = jax.random.split(key, 6)
        s = 1.0 / np.sqrt(QUERY_DIM)
        x = jax.random.normal(ks[0], (B, N, QUERY_DIM), dtype=jnp.float32)
        adjacency_mask = jax.random.randint(ks[1], (B, N, N), 0, 2) > 0
        Wq = jax.random.normal(ks[2], (QUERY_DIM, INNER), dtype=jnp.float32) * s
        Wk = jax.random.normal(ks[3], (QUERY_DIM, INNER), dtype=jnp.float32) * s
        Wv = jax.random.normal(ks[4], (QUERY_DIM, INNER), dtype=jnp.float32) * s
        Wo = jax.random.normal(ks[5], (INNER, QUERY_DIM), dtype=jnp.float32) * (1.0 / np.sqrt(INNER))
        bo = jnp.zeros((QUERY_DIM,), dtype=jnp.float32)
        return {'x': x, 'adjacency_mask': adjacency_mask, 'Wq': Wq, 'Wk': Wk, 'Wv': Wv, 'Wo': Wo, 'bo': bo}
    _L0_gnn_all = _L0_gnn_setup()
    _L0_gnn_in = {k: v for k, v in _L0_gnn_all.items() if k in ('Wq', 'Wk', 'Wv', 'Wo', 'bo')}
    del _L0_gnn_all

    def _L1_gnn_setup():
        import jax, jax.numpy as jnp
        import numpy as np
        B, N, IN, OUT, H = (16, 512, 256, 256, 4)
        key = jax.random.key(seed)
        ks = jax.random.split(key, 10)
        s = 0.03
        return {'h': jax.random.normal(ks[0], (B, N, IN), jnp.float32), 'adj': jax.random.randint(ks[1], (B, N, N), 0, 2) > 0, 'W': jax.random.normal(ks[2], (H, OUT, IN), jnp.float32) * s, 'bW': jax.random.normal(ks[3], (H, OUT), jnp.float32) * s, 'attn': jax.random.normal(ks[4], (H, OUT, OUT), jnp.float32) * s, 'A_w': jax.random.normal(ks[5], (OUT, OUT * H), jnp.float32) * s, 'fc_w': jax.random.normal(ks[6], (OUT, IN), jnp.float32) * s, 'g1_w': jax.random.normal(ks[7], (OUT, OUT), jnp.float32) * s, 'g2_w': jax.random.normal(ks[8], (OUT, OUT), jnp.float32) * s, 'gbias': jax.random.normal(ks[9], (OUT,), jnp.float32) * s}
    _L1_gnn_all = _L1_gnn_setup()
    _L1_gnn_in = {k: v for k, v in _L1_gnn_all.items() if k in ('W', 'bW', 'attn', 'A_w', 'fc_w', 'g1_w', 'g2_w', 'gbias')}
    del _L1_gnn_all

    def _L2_gnn_setup():
        import jax, jax.numpy as jnp
        import numpy as np
        HEAD_NUM = 8
        THRESHOLD = 0.1
        NEG = -10000000000.0
        COS_EPS = 1e-08
        B, S, D = (8, 512, 256)
        D_OUT = 256
        key = jax.random.key(seed)
        ks = jax.random.split(key, 12)
        embs = jax.random.normal(ks[0], (B, S, D), dtype=jnp.float32)
        lengths = jax.random.randint(ks[1], (B,), S // 2, S + 1)
        pad = jnp.arange(S)[None, :] >= lengths[:, None]
        score_mask = pad[:, :, None] | pad[:, None, :]
        sc = 1.0 / np.sqrt(D)
        mk = lambda k, shp: jax.random.normal(k, shp, dtype=jnp.float32) * sc
        return {'embs': embs, 'score_mask': score_mask, 'map_w': mk(ks[2], (D, D)), 'map_b': jnp.zeros((D,), jnp.float32), 'q_w': mk(ks[3], (D, D)), 'q_b': jnp.zeros((D,), jnp.float32), 'k_w': mk(ks[4], (D, D)), 'k_b': jnp.zeros((D,), jnp.float32), 'gcn_map_w': mk(ks[5], (D_OUT, D)), 'gcn_map_b': jnp.zeros((D_OUT,), jnp.float32), 'gcn_W': jax.random.normal(ks[6], (D_OUT // HEAD_NUM, D_OUT // HEAD_NUM), dtype=jnp.float32) * (1.0 / np.sqrt(D_OUT // HEAD_NUM))}
    _L2_gnn_all = _L2_gnn_setup()
    _L2_gnn_in = {k: v for k, v in _L2_gnn_all.items() if k in ('map_w', 'map_b', 'q_w', 'q_b', 'k_w', 'k_b', 'gcn_map_w', 'gcn_map_b', 'gcn_W')}
    del _L2_gnn_all

    def _L3_gnn_setup():
        import jax, jax.numpy as jnp
        import numpy as np
        QUERY_DIM = 256
        HEADS = 4
        DIM_HEAD = 64
        INNER = HEADS * DIM_HEAD
        B, N = (4, 1024)
        key = jax.random.key(seed)
        ks = jax.random.split(key, 6)
        s = 1.0 / np.sqrt(QUERY_DIM)
        x = jax.random.normal(ks[0], (B, N, QUERY_DIM), dtype=jnp.float32)
        adjacency_mask = jax.random.randint(ks[1], (B, N, N), 0, 2) > 0
        Wq = jax.random.normal(ks[2], (QUERY_DIM, INNER), dtype=jnp.float32) * s
        Wk = jax.random.normal(ks[3], (QUERY_DIM, INNER), dtype=jnp.float32) * s
        Wv = jax.random.normal(ks[4], (QUERY_DIM, INNER), dtype=jnp.float32) * s
        Wo = jax.random.normal(ks[5], (INNER, QUERY_DIM), dtype=jnp.float32) * (1.0 / np.sqrt(INNER))
        bo = jnp.zeros((QUERY_DIM,), dtype=jnp.float32)
        return {'x': x, 'adjacency_mask': adjacency_mask, 'Wq': Wq, 'Wk': Wk, 'Wv': Wv, 'Wo': Wo, 'bo': bo}
    _L3_gnn_all = _L3_gnn_setup()
    _L3_gnn_in = {k: v for k, v in _L3_gnn_all.items() if k in ('Wq', 'Wk', 'Wv', 'Wo', 'bo')}
    del _L3_gnn_all
    return {'x': x, 'adj': adj, 'L0_gnn_Wq': _L0_gnn_in['Wq'], 'L0_gnn_Wk': _L0_gnn_in['Wk'], 'L0_gnn_Wv': _L0_gnn_in['Wv'], 'L0_gnn_Wo': _L0_gnn_in['Wo'], 'L0_gnn_bo': _L0_gnn_in['bo'], 'L1_gnn_W': _L1_gnn_in['W'], 'L1_gnn_bW': _L1_gnn_in['bW'], 'L1_gnn_attn': _L1_gnn_in['attn'], 'L1_gnn_A_w': _L1_gnn_in['A_w'], 'L1_gnn_fc_w': _L1_gnn_in['fc_w'], 'L1_gnn_g1_w': _L1_gnn_in['g1_w'], 'L1_gnn_g2_w': _L1_gnn_in['g2_w'], 'L1_gnn_gbias': _L1_gnn_in['gbias'], 'L2_gnn_map_w': _L2_gnn_in['map_w'], 'L2_gnn_map_b': _L2_gnn_in['map_b'], 'L2_gnn_q_w': _L2_gnn_in['q_w'], 'L2_gnn_q_b': _L2_gnn_in['q_b'], 'L2_gnn_k_w': _L2_gnn_in['k_w'], 'L2_gnn_k_b': _L2_gnn_in['k_b'], 'L2_gnn_gcn_map_w': _L2_gnn_in['gcn_map_w'], 'L2_gnn_gcn_map_b': _L2_gnn_in['gcn_map_b'], 'L2_gnn_gcn_W': _L2_gnn_in['gcn_W'], 'L3_gnn_Wq': _L3_gnn_in['Wq'], 'L3_gnn_Wk': _L3_gnn_in['Wk'], 'L3_gnn_Wv': _L3_gnn_in['Wv'], 'L3_gnn_Wo': _L3_gnn_in['Wo'], 'L3_gnn_bo': _L3_gnn_in['bo']}

def reference(x, adj, L0_gnn_Wq, L0_gnn_Wk, L0_gnn_Wv, L0_gnn_Wo, L0_gnn_bo, L1_gnn_W, L1_gnn_bW, L1_gnn_attn, L1_gnn_A_w, L1_gnn_fc_w, L1_gnn_g1_w, L1_gnn_g2_w, L1_gnn_gbias, L2_gnn_map_w, L2_gnn_map_b, L2_gnn_q_w, L2_gnn_q_b, L2_gnn_k_w, L2_gnn_k_b, L2_gnn_gcn_map_w, L2_gnn_gcn_map_b, L2_gnn_gcn_W, L3_gnn_Wq, L3_gnn_Wk, L3_gnn_Wv, L3_gnn_Wo, L3_gnn_bo):
    import jax
    import jax.numpy as jnp

    def _L0_gnn_ref(x, adjacency_mask, Wq, Wk, Wv, Wo, bo):
        import jax, jax.numpy as jnp
        import numpy as np
        QUERY_DIM = 256
        HEADS = 4
        DIM_HEAD = 64
        INNER = HEADS * DIM_HEAD
        B, N = (4, 1024)
        scale = DIM_HEAD ** (-0.5)

        def split_heads(t):
            b, n, _ = t.shape
            return t.reshape(b, n, HEADS, DIM_HEAD).transpose(0, 2, 1, 3)
        q = split_heads(x @ Wq)
        k = split_heads(x @ Wk)
        v = split_heads(x @ Wv)
        sim = jnp.einsum('bhid,bhjd->bhij', q, k) * scale
        neg = -jnp.finfo(sim.dtype).max
        sim = jnp.where(adjacency_mask[:, None, :, :], sim, neg)
        attn = jax.nn.softmax(sim, axis=-1)
        out = jnp.einsum('bhij,bhjd->bhid', attn, v)
        out = out.transpose(0, 2, 1, 3).reshape(x.shape[0], x.shape[1], INNER)
        return out @ Wo + bo

    def _L1_gnn_ref(h, adj, W, bW, attn, A_w, fc_w, g1_w, g2_w, gbias):
        import jax, jax.numpy as jnp
        import numpy as np
        B, N, IN, OUT, H = (16, 512, 256, 256, 4)
        Wh = jnp.einsum('bni,hoi->bhno', h, W) + bW[None, :, None, :]
        e = jnp.einsum('bhno,hop->bhnp', Wh, attn)
        scores = jnp.einsum('bhnp,bhmp->bhnm', e, Wh)
        A_mat = jnp.tanh(jnp.where(adj[:, None, :, :], scores, 0.0))
        hp = jax.nn.relu(jnp.einsum('bhnm,bhmo->bhno', A_mat, Wh))
        cat = jnp.transpose(hp, (0, 2, 1, 3)).reshape(hp.shape[0], hp.shape[2], -1)
        ha = cat @ A_w.T
        hf = h @ fc_w.T
        coeff = jax.nn.sigmoid(hf @ g1_w.T + ha @ g2_w.T + gbias)
        return hf * coeff + ha * (1.0 - coeff)

    def _L2_gnn_ref(embs, score_mask, map_w, map_b, q_w, q_b, k_w, k_b, gcn_map_w, gcn_map_b, gcn_W):
        import jax, jax.numpy as jnp
        import numpy as np
        HEAD_NUM = 8
        THRESHOLD = 0.1
        NEG = -10000000000.0
        COS_EPS = 1e-08
        B, S, D = (8, 512, 256)
        D_OUT = 256
        b, s, d = embs.shape
        h, dk = (HEAD_NUM, d // HEAD_NUM)
        sm = score_mask[:, None, :, :]
        keep = (~sm[..., 0:1]).astype(embs.dtype)
        m = embs @ map_w.T + map_b
        sem = m.reshape(b, s, h, dk).transpose(0, 2, 1, 3)
        norm = jnp.maximum(jnp.linalg.norm(sem, axis=-1, keepdims=True), COS_EPS)
        n = sem / norm
        cos = jnp.einsum('bhsd,bhtd->bhst', n, n)
        cos = cos * (~sm).astype(cos.dtype)
        cos_adj = (cos > THRESHOLD).astype(embs.dtype)
        q = (m @ q_w.T + q_b).reshape(b, s, h, dk).transpose(0, 2, 1, 3)
        k = (m @ k_w.T + k_b).reshape(b, s, h, dk).transpose(0, 2, 1, 3)
        scores = jnp.einsum('bhsd,bhtd->bhst', q, k) / jnp.sqrt(jnp.asarray(dk, embs.dtype))
        scores = jnp.where(sm, NEG, scores)
        p_attn = jax.nn.softmax(scores, axis=-1) * keep
        adj = cos_adj * p_attn
        hk = gcn_map_w.shape[0] // h
        sem_h = (embs @ gcn_map_w.T + gcn_map_b).reshape(b, s, h, hk).transpose(2, 0, 1, 3)
        adj_h = adj.transpose(1, 0, 2, 3)
        Ax = jnp.einsum('hbst,hbtd->hbsd', adj_h, sem_h)
        AxW = Ax @ gcn_W.T
        denom = adj_h.sum(-1, keepdims=True) + 1.0
        out = jax.nn.relu(AxW / denom)
        out = out.transpose(1, 2, 0, 3).reshape(b, s, h * hk)
        return out

    def _L3_gnn_ref(x, adjacency_mask, Wq, Wk, Wv, Wo, bo):
        import jax, jax.numpy as jnp
        import numpy as np
        QUERY_DIM = 256
        HEADS = 4
        DIM_HEAD = 64
        INNER = HEADS * DIM_HEAD
        B, N = (4, 1024)
        scale = DIM_HEAD ** (-0.5)

        def split_heads(t):
            b, n, _ = t.shape
            return t.reshape(b, n, HEADS, DIM_HEAD).transpose(0, 2, 1, 3)
        q = split_heads(x @ Wq)
        k = split_heads(x @ Wk)
        v = split_heads(x @ Wv)
        sim = jnp.einsum('bhid,bhjd->bhij', q, k) * scale
        neg = -jnp.finfo(sim.dtype).max
        sim = jnp.where(adjacency_mask[:, None, :, :], sim, neg)
        attn = jax.nn.softmax(sim, axis=-1)
        out = jnp.einsum('bhij,bhjd->bhid', attn, v)
        out = out.transpose(0, 2, 1, 3).reshape(x.shape[0], x.shape[1], INNER)
        return out @ Wo + bo
    x = _layernorm(x + _L0_gnn_ref(x, adj, L0_gnn_Wq, L0_gnn_Wk, L0_gnn_Wv, L0_gnn_Wo, L0_gnn_bo), axis=-1)
    x = _layernorm(x + _L1_gnn_ref(x, adj, L1_gnn_W, L1_gnn_bW, L1_gnn_attn, L1_gnn_A_w, L1_gnn_fc_w, L1_gnn_g1_w, L1_gnn_g2_w, L1_gnn_gbias), axis=-1)
    x = _layernorm(x + _L2_gnn_ref(x, adj, L2_gnn_map_w, L2_gnn_map_b, L2_gnn_q_w, L2_gnn_q_b, L2_gnn_k_w, L2_gnn_k_b, L2_gnn_gcn_map_w, L2_gnn_gcn_map_b, L2_gnn_gcn_W), axis=-1)
    x = _layernorm(x + _L3_gnn_ref(x, adj, L3_gnn_Wq, L3_gnn_Wk, L3_gnn_Wv, L3_gnn_Wo, L3_gnn_bo), axis=-1)
    return x

_drawn_inputs = setup_inputs


def setup_inputs(seed=0):
    import zlib

    import numpy as np

    out = dict(_drawn_inputs(seed))
    spreads = {'L0_gnn_bo': (0.0, 0.1),
     'L2_gnn_map_b': (0.0, 0.788),
     'L2_gnn_q_b': (0.0, 0.8),
     'L2_gnn_k_b': (0.0, 0.8),
     'L2_gnn_gcn_map_b': (0.0, 0.294),
     'L3_gnn_bo': (0.0, 0.1)}
    factors = {'L1_gnn_gbias': 5.95}
    for name, (base, spread) in spreads.items():
        noise = np.random.default_rng([zlib.crc32(name.encode()), seed]).standard_normal(out[name].shape)
        drawn = base * np.exp(spread * noise) if base else spread * noise
        out[name] = jnp.asarray(drawn.astype(out[name].dtype))
    for name, factor in factors.items():
        out[name] = (out[name] * factor).astype(out[name].dtype)
    return out
```

```python
from contextlib import ExitStack

import numpy as np
import concourse.bass as bass
import concourse.mybir as mybir
from concourse.alu_op_type import AluOpType as ALU

ACT = mybir.ActivationFunctionType
AX_X = mybir.AxisListType.X
F32 = mybir.dt.float32
BF16 = mybir.dt.bfloat16
U8 = mybir.dt.uint8

GRAPHS, NODES, DIM = 32, 256, 256
P = 128
T = NODES // P
HA, DHA = 4, 64
HG = 4
HS, DHS = 8, 32
COS_MIN = 0.1
COS_EPS = 1e-8
LN_EPS = 1e-5
MASKED = -3.3e38
MAX_FLOOR = -1e30
BANK = 512

SCHEDULE = [
    ("a_x_t", "b_x_t"),
    ("a_qkv", "b_project"),
    ("a_scores", "b_unit_t"),
    (None, "b_head_0"),
    ("a_probs_01", "b_head_1"),
    ("a_probs_23", "b_head_2"),
    ("a_values", "b_head_3"),
    ("a_out", "b_head_4"),
    (None, "b_head_5"),
    ("g_x_t", "b_head_6"),
    ("g_wh", "b_head_7"),
    ("g_0", "b_head_8"),
    ("g_1", "b_head_9"),
    ("g_2", "b_out"),
    ("g_3", None),
    ("g_4", "d_x_t"),
    ("g_5", "d_qkv"),
    ("g_6", "d_scores"),
    ("g_ha", "d_probs_01"),
    ("g_ha_t", "d_probs_23"),
    ("g_gate", "d_values"),
    (None, "d_out"),
]


class Signal:

    def __init__(self, ctx, nc, name, per=1):
        self.sem = ctx.enter_context(nc.semaphore(name))
        self.per = per

    def at(self, g, k=1):
        return g * self.per + k

    def all(self, g):
        return g * self.per + self.per


def apart(eng):
    eng.nop(nofuse=True)


def later(g):
    return not isinstance(g, int) or g > 0


class Names:
    pass


def norm_signals(ctx, nc, name):
    N = Names()
    N.sum = Signal(ctx, nc, f"{name}_sum")
    N.stats = Signal(ctx, nc, f"{name}_stats")
    N.var = Signal(ctx, nc, f"{name}_var")
    N.eps = Signal(ctx, nc, f"{name}_eps")
    N.rstd = Signal(ctx, nc, f"{name}_rstd")
    N.out = Signal(ctx, nc, f"{name}_out")
    return N


def norm_buffers(ctx, nc, N, name):
    N.r = ctx.enter_context(nc.sbuf_tensor(f"{name}_r", [P, T, DIM], F32))
    N.st = ctx.enter_context(nc.sbuf_tensor(f"{name}_st", [P, T, 6], F32))
    N.mv = ctx.enter_context(nc.sbuf_tensor(f"{name}_mv", [P, T, 2], F32))
    N.ve = ctx.enter_context(nc.sbuf_tensor(f"{name}_ve", [P, T], F32))
    N.rs = ctx.enter_context(nc.sbuf_tensor(f"{name}_rs", [P, T], F32))


def dve_norm_stats(dve, N, g):
    dve.wait_ge(N.sum.sem, N.sum.at(g))
    for it in range(T):
        last = dve.bn_stats(N.st[:, it, :], N.r[:, it, :])
    last.then_inc(N.stats.sem, 1)
    dve.wait_ge(N.stats.sem, N.stats.at(g))
    apart(dve)
    for it in range(T):
        last = dve.bn_aggr(N.mv[:, it, :], N.st[:, it, :])
    last.then_inc(N.var.sem, 1)


def dve_norm_out(dve, N, g, out):
    dve.wait_ge(N.rstd.sem, N.rstd.at(g))
    for it in range(T):
        last = dve.tensor_scalar(out[:, it, :], N.r[:, it, :], N.mv[:, it, 0:1], N.rs[:, it:it + 1],
                                 ALU.subtract, ALU.mult)
    last.then_inc(N.out.sem, 1)


def pool_norm(pool, N, C, g):
    pool.wait_ge(N.var.sem, N.var.at(g))
    apart(pool)
    pool.tensor_scalar(N.ve[:, :], N.mv[:, :, 1], LN_EPS, None, ALU.add).then_inc(N.eps.sem, 1)
    pool.wait_ge(N.eps.sem, N.eps.at(g))
    pool.tensor_tensor(N.rs[:, :], N.ve[:, :], C.minus_half[:, 0:T], ALU.pow).then_inc(N.rstd.sem, 1)


def attention_layer(ctx, nc, name, banks):
    L = Names()
    L.banks = banks
    L.x_t_psum = Signal(ctx, nc, f"{name}_x_t_psum")
    L.x_t_sb = Signal(ctx, nc, f"{name}_x_t_sb")
    L.qkv_psum = Signal(ctx, nc, f"{name}_qkv_psum", 3)
    L.qk_sb = Signal(ctx, nc, f"{name}_qk_sb", 2)
    L.v_sb = Signal(ctx, nc, f"{name}_v_sb")
    L.s_psum = Signal(ctx, nc, f"{name}_s_psum", HA)
    L.max = Signal(ctx, nc, f"{name}_max", HA)
    L.shift = Signal(ctx, nc, f"{name}_shift", HA)
    L.exp = Signal(ctx, nc, f"{name}_exp", HA)
    L.inv = Signal(ctx, nc, f"{name}_inv", HA)
    L.p = Signal(ctx, nc, f"{name}_p", HA)
    L.p_t_psum = Signal(ctx, nc, f"{name}_p_t_psum", HA)
    L.p_t_act = Signal(ctx, nc, f"{name}_p_t_act", HA // 2)
    L.p_t_dve = Signal(ctx, nc, f"{name}_p_t_dve", HA // 2)
    L.o_psum = Signal(ctx, nc, f"{name}_o_psum")
    L.o_sb = Signal(ctx, nc, f"{name}_o_sb")
    L.y_psum = Signal(ctx, nc, f"{name}_y_psum")
    L.x_bias = Signal(ctx, nc, f"{name}_x_bias")
    L.mask = Signal(ctx, nc, f"{name}_mask")
    L.norm = norm_signals(ctx, nc, name)

    def sb(what, shape, dt=F32):
        return ctx.enter_context(nc.sbuf_tensor(f"{name}_{what}", shape, dt))

    L.xt = sb("xt", [P, T, NODES])
    L.qt = sb("qt", [P, T, NODES])
    L.kt = sb("kt", [P, T, NODES])
    L.v = sb("v", [P, T, DIM])
    L.mx = sb("mx", [P, HA, T])
    L.sh = sb("sh", [P, HA, T])
    L.sums = sb("sums", [P, HA, T])
    L.iv = sb("iv", [P, HA, T])
    L.e = sb("e", [P, HA, T, NODES])
    L.pt = sb("pt", [P, HA, T, NODES])
    L.ot = sb("ot", [P, T, NODES])
    L.xb = sb("xb", [P, T, DIM])
    L.add = sb("add", [P, T, NODES], BF16)
    L.wq, L.wk, L.wv, L.wo = (sb(f"w{n}", [P, T, DIM]) for n in "qkvo")
    L.bo = sb("bo", [P, DIM])
    norm_buffers(ctx, nc, L.norm, name)
    return L


def view(bank, inner=NODES):
    return bank[:, :].rearrange("p (a n) -> p a n", n=inner)


def pe_transpose_rows(pe, out_bank, rows, ident):
    for kc in range(T):
        for it in range(T):
            last = pe.transpose(out_bank[:, kc * NODES + it * P:kc * NODES + (it + 1) * P],
                                rows[:, it, kc * P:(kc + 1) * P], ident[:, :])
    return last


def pe_feature_major(pe, out_bank, w, x_t):
    for jt in range(T):
        for kc in range(T):
            last = pe.matmul(out_bank[:, jt * NODES:(jt + 1) * NODES], w[:, kc, jt * P:(jt + 1) * P],
                             x_t[:, kc, :], start=(kc == 0), stop=(kc == T - 1))
    return last


def pe_node_major(pe, out_bank, x_t, w):
    for it in range(T):
        for kc in range(T):
            last = pe.matmul(out_bank[:, it * DIM:(it + 1) * DIM], x_t[:, kc, it * P:(it + 1) * P],
                             w[:, kc, :], start=(kc == 0), stop=(kc == T - 1))
    return last


def pe_attention(pe, L, C, x):
    B = L.banks

    def x_t(g):
        pe_transpose_rows(pe, B[0], x, C.ident).then_inc(L.x_t_psum.sem, 1)

    def qkv(g):
        pe.wait_ge(L.x_t_sb.sem, L.x_t_sb.at(g))
        pe_feature_major(pe, B[1], L.wq, L.xt).then_inc(L.qkv_psum.sem, 1)
        pe_feature_major(pe, B[2], L.wk, L.xt).then_inc(L.qkv_psum.sem, 1)
        pe_node_major(pe, B[3], L.xt, L.wv).then_inc(L.qkv_psum.sem, 1)

    def scores(g):
        pe.wait_ge(L.mask.sem, L.mask.at(g))
        pe.wait_ge(L.qk_sb.sem, L.qk_sb.at(g, 2))
        pe.wait_ge(L.v_sb.sem, L.v_sb.at(g))
        for h in range(HA):
            rows = slice(DHA * (h % 2), DHA * (h % 2) + DHA)
            for it in range(T):
                out = B[h][:, it * NODES:(it + 1) * NODES]
                pe.matmul(out, C.ident_bf[:, :], L.add[:, it, :], start=True, stop=False)
                last = pe.matmul(out, L.qt[rows, h // 2, it * P:(it + 1) * P], L.kt[rows, h // 2, :],
                                 start=False, stop=True)
            last.then_inc(L.s_psum.sem, 1)

    def probs(g, heads):
        for h in heads:
            pe.wait_ge(L.p.sem, L.p.at(g, h + 1))
            for jt in range(T):
                for it in range(T):
                    last = pe.transpose(B[h][:, jt * NODES + it * P:jt * NODES + (it + 1) * P],
                                        L.e[:, h, it, jt * P:(jt + 1) * P], C.ident[:, :])
            last.then_inc(L.p_t_psum.sem, 1)

    def values(g):
        for pair in range(HA // 2):
            pe.wait_ge(L.p_t_act.sem, L.p_t_act.at(g, pair + 1))
            pe.wait_ge(L.p_t_dve.sem, L.p_t_dve.at(g, pair + 1))
            for jt in range(T):
                for half in range(2):
                    h = 2 * pair + half
                    last = pe.matmul(B[0][half * DHA:(half + 1) * DHA, pair * NODES:(pair + 1) * NODES],
                                     L.v[:, jt, h * DHA:(h + 1) * DHA], L.pt[:, h, jt, :],
                                     start=(jt == 0), stop=(jt == T - 1))
        last.then_inc(L.o_psum.sem, 1)

    def out(g):
        pe.wait_ge(L.o_sb.sem, L.o_sb.at(g))
        pe_node_major(pe, B[1], L.ot, L.wo).then_inc(L.y_psum.sem, 1)

    return x_t, qkv, scores, probs, values, out


def act_attention(act, L):
    B = L.banks

    def x_t(g):
        act.wait_ge(L.x_t_psum.sem, L.x_t_psum.at(g))
        act.activation(L.xt[:, :, :], view(B[0]), ACT.Copy).then_inc(L.x_t_sb.sem, 1)

    def qkv(g):
        for n, dst in enumerate((L.qt, L.kt)):
            act.wait_ge(L.qkv_psum.sem, L.qkv_psum.at(g, n + 1))
            act.activation(dst[:, :, :], view(B[1 + n]), ACT.Copy).then_inc(L.qk_sb.sem, 1)

    def scores(g):
        for h in range(HA):
            if later(g):
                act.wait_ge(L.p_t_psum.sem, L.p_t_psum.at(g - 1, h + 1))
            act.wait_ge(L.shift.sem, L.shift.at(g, h + 1))
            for it in range(T):
                last = act.activation(L.e[:, h, it, :], B[h][:, it * NODES:(it + 1) * NODES], ACT.Exp,
                                      bias=L.sh[:, h, it:it + 1], scale=DHA ** -0.5,
                                      accum_out=L.sums[:, h, it:it + 1])
            last.then_inc(L.exp.sem, 1)

    def probs(g, heads):
        for h in heads:
            if h % 2 == 0:
                if later(g):
                    act.wait_ge(L.o_psum.sem, L.o_psum.all(g - 1))
                act.wait_ge(L.p_t_psum.sem, L.p_t_psum.at(g, h + 1))
                act.activation(L.pt[:, h, :, :], view(B[h]), ACT.Copy).then_inc(L.p_t_act.sem, 1)

    def values(g):
        act.wait_ge(L.o_psum.sem, L.o_psum.at(g))
        act.activation(L.ot[:, :, :], view(B[0]), ACT.Copy).then_inc(L.o_sb.sem, 1)

    return x_t, qkv, scores, probs, values


def dve_attention(dve, L):
    B = L.banks

    def qkv(g):
        if later(g):
            dve.wait_ge(L.o_psum.sem, L.o_psum.all(g - 1))
        dve.wait_ge(L.qkv_psum.sem, L.qkv_psum.at(g, 3))
        dve.tensor_copy(L.v[:, :, :], view(B[3])).then_inc(L.v_sb.sem, 1)

    def scores(g):
        for h in range(HA):
            if later(g):
                dve.wait_ge(L.shift.sem, L.shift.at(g - 1, h + 1))
            dve.wait_ge(L.s_psum.sem, L.s_psum.at(g, h + 1))
            dve.reduce_max(L.mx[:, h, :], view(B[h]), AX_X).then_inc(L.max.sem, 1)

    def probs(g, heads):
        for h in heads:
            if h % 2 == 1:
                if later(g):
                    dve.wait_ge(L.o_psum.sem, L.o_psum.all(g - 1))
                dve.wait_ge(L.p_t_psum.sem, L.p_t_psum.at(g, h + 1))
                dve.tensor_copy(L.pt[:, h, :, :], view(B[h])).then_inc(L.p_t_dve.sem, 1)

    def finish(g):
        dve.wait_ge(L.x_bias.sem, L.x_bias.at(g))
        dve.wait_ge(L.y_psum.sem, L.y_psum.at(g))
        dve.tensor_tensor(L.norm.r[:, :, :], view(B[1]), L.xb[:, :, :], ALU.add).then_inc(L.norm.sum.sem, 1)
        dve_norm_stats(dve, L.norm, g)

    return qkv, scores, probs, finish


def pool_attention(pool, L, C):
    def scores(g):
        for h in range(HA):
            if later(g):
                pool.wait_ge(L.exp.sem, L.exp.at(g - 1, h + 1))
            pool.wait_ge(L.max.sem, L.max.at(g, h + 1))
            apart(pool)
            pool.tensor_scalar(L.sh[:, h, :], L.mx[:, h, :], -(DHA ** -0.5), None, ALU.mult)\
                .then_inc(L.shift.sem, 1)

    def normalise(g):
        for h in range(HA):
            pool.wait_ge(L.exp.sem, L.exp.at(g, h + 1))
            pool.tensor_tensor(L.iv[:, h, :], L.sums[:, h, :], C.minus_one[:, 0:T], ALU.pow)\
                .then_inc(L.inv.sem, 1)
            pool.wait_ge(L.inv.sem, L.inv.at(g, h + 1))
            apart(pool)
            for it in range(T):
                last = pool.tensor_scalar(L.e[:, h, it, :], L.e[:, h, it, :], L.iv[:, h, it:it + 1],
                                          None, ALU.mult)
            last.then_inc(L.p.sem, 1)

    def finish(g):
        pool_norm(pool, L.norm, C, g)

    return scores, normalise, finish


def pool_attention_inputs(pool, L, g, x, adj):
    if later(g):
        pool.wait_ge(L.s_psum.sem, L.s_psum.all(g - 1))
    apart(pool)
    pool.tensor_scalar(L.add[:, :, :], adj[:, :, :], 1.0, -MASKED, ALU.subtract, ALU.mult)\
        .then_inc(L.mask.sem, 1)
    if later(g):
        pool.wait_ge(L.norm.sum.sem, L.norm.sum.all(g - 1))
    for it in range(T):
        last = pool.tensor_tensor(L.xb[:, it, :], x[:, it, :], L.bo[:, :], ALU.add)
    last.then_inc(L.x_bias.sem, 1)


def build(nc, d, out_dram):
    with ExitStack() as ctx:
        def sb(name, shape, dt=F32):
            return ctx.enter_context(nc.sbuf_tensor(name, shape, dt))

        def signal(name, per=1):
            return Signal(ctx, nc, name, per)

        banks = [ctx.enter_context(nc.psum_tensor(f"bank{i}", [P, BANK], F32)) for i in range(8)]
        BA, BB = banks[:4], banks[4:]

        C = Names()
        C.ident, C.ident_bf = sb("ident", [P, P]), sb("ident_bf", [P, P], BF16)
        C.ones, C.minus_one, C.minus_half = sb("ones", [P, P]), sb("minus_one", [P, 16]), sb("minus_half", [P, 16])

        x_in, x_loaded = sb("x_in", [P, T, DIM]), signal("x_loaded", 16)
        adj_a, adj_a_loaded = sb("adj_a", [P, T, NODES], U8), signal("adj_a_loaded", 16)
        adj_b, adj_b_loaded = sb("adj_b", [P, T, NODES], U8), signal("adj_b_loaded", 16)
        x1, x2, x3, x4 = (sb(f"x{n}", [P, T, DIM]) for n in (1, 2, 3, 4))
        stored = signal("stored", 16)

        A = attention_layer(ctx, nc, "l0", BA)
        D = attention_layer(ctx, nc, "l3", BB)

        G = Names()
        G.x_t_psum, G.x_t_sb = signal("l1_x_t_psum"), signal("l1_x_t_sb")
        G.adj_psum, G.adj_sb = signal("l1_adj_psum"), signal("l1_adj_sb")
        G.adj_bf_ready = signal("l1_adj_bf")
        G.wh_psum, G.wh_sb = signal("l1_wh_psum", 4), signal("l1_wh_sb", 4)
        G.c_psum, G.c_sb = signal("l1_c_psum"), signal("l1_c_sb")
        G.z_psum, G.z_sb = signal("l1_z_psum", HG), signal("l1_z_sb", HG)
        G.s_psum, G.tanh = signal("l1_s_psum", HG), signal("l1_tanh", HG)
        G.a = signal("l1_a", HG)
        G.p_psum, G.hp = signal("l1_p_psum", HG), signal("l1_hp", HG)
        G.ha_psum, G.ha_sb = signal("l1_ha_psum"), signal("l1_ha_sb")
        G.ha_t_psum, G.ha_t_sb = signal("l1_ha_t_psum"), signal("l1_ha_t_sb")
        G.gate_psum, G.pre, G.gate = signal("l1_gate_psum", T), signal("l1_pre", T), signal("l1_gate", T)
        G.diff, G.part, G.x_ha_done = signal("l1_diff", T), signal("l1_part", T), signal("l1_x_ha")
        G.norm = norm_signals(ctx, nc, "l1")
        norm_buffers(ctx, nc, G.norm, "l1")
        G.xt = sb("g_xt", [P, T, NODES])
        G.adj_bf, G.adj_t = sb("g_adj_bf", [P, T, NODES], BF16), sb("g_adj_t", [P, T, NODES])
        G.wh = sb("g_wh", [P, T, HG * DIM])
        G.c = sb("g_c", [P, T, HG])
        G.zt, G.th = A.e[:, 0:2], A.e[:, 2:4]
        G.am = sb("g_am", [P, 2, T, NODES])
        G.hpt = A.pt
        G.ha, G.hat = sb("g_ha", [P, T, DIM]), sb("g_hat", [P, T, NODES])
        G.x_ha, G.pr, G.gt, G.df, G.pa = (sb(f"g_{n}", [P, T, DIM]) for n in ("x_ha", "pr", "gt", "df", "pa"))
        G.w_t = sb("g_w_t", [P, T, HG * DIM])
        G.w_z = sb("g_w_z", [P, HG, T, DIM])
        G.w_a = sb("g_w_a", [P, HG * T, DIM])
        G.w_fg = sb("g_w_fg", [P, T, 2 * DIM])
        G.w_g2 = sb("g_w_g2", [P, T, DIM])
        G.b_wh, G.b_gate = sb("g_b_wh", [P, HG * DIM]), sb("g_b_gate", [P, DIM])
        G.b_z, G.w_c, G.b_c = sb("g_b_z", [P, T, HG]), sb("g_w_c", [P, T, HG]), sb("g_b_c", [P, HG])

        S = Names()
        S.x_t_psum, S.x_t_sb = signal("l2_x_t_psum"), signal("l2_x_t_sb")
        S.m_psum, S.qk_psum, S.sem_psum = signal("l2_m_psum"), signal("l2_qk_psum", 2), signal("l2_sem_psum")
        S.m_sb, S.sem_sb, S.qk_sb = signal("l2_m_sb"), signal("l2_sem_sb"), signal("l2_qk_sb", 2)
        S.square, S.sumsq, S.floor, S.inorm, S.unit = (signal(f"l2_{n}") for n in ("square", "sumsq", "floor", "inorm", "unit"))
        S.unit_psum, S.unit_sb = signal("l2_unit_psum"), signal("l2_unit_sb")
        S.mask, S.keep = signal("l2_mask"), signal("l2_keep")
        S.s_psum, S.cos_psum = signal("l2_s_psum", HS), signal("l2_cos_psum", HS)
        S.max, S.shift, S.exp = signal("l2_max", HS), signal("l2_shift", HS), signal("l2_exp", HS)
        S.cut = signal("l2_cut", HS)
        S.f = [signal(f"l2_f{n}", HS) for n in range(4)]
        S.a = signal("l2_a", HS)
        S.a_t_psum, S.a_t_act, S.a_t_dve = signal("l2_a_t_psum", HS), signal("l2_a_t_act", HS // 2), signal("l2_a_t_dve", HS // 2)
        S.o_psum, S.o_sb = signal("l2_o_psum", 2), signal("l2_o_sb", 2)
        S.y_psum = signal("l2_y_psum")
        S.norm = norm_signals(ctx, nc, "l2")
        norm_buffers(ctx, nc, S.norm, "l2")
        S.xt, S.qt, S.kt, S.ut = (sb(f"s_{n}", [P, T, NODES]) for n in ("xt", "qt", "kt", "ut"))
        S.m, S.sem, S.sq, S.u = (sb(f"s_{n}", [P, T, DIM]) for n in ("m", "sem", "sq", "u"))
        S.ss, S.fl, S.inv = (sb(f"s_{n}", [P, T * HS]) for n in ("ss", "fl", "inv"))
        S.add, S.kp, S.drop = sb("s_add", [P, T, NODES], BF16), sb("s_kp", [P, T]), sb("s_drop", [P, T])
        S.mx, S.sh, S.sums, S.dsum, S.f1, S.f2, S.f3, S.fac = (
            sb(f"s_{n}", [P, HS, T]) for n in ("mx", "sh", "sums", "dsum", "f1", "f2", "f3", "fac"))
        S.e, S.cutp, S.at = D.pt[:, 0:2], D.pt[:, 2:4], D.e
        S.ot = sb("s_ot", [P, 2, NODES])
        S.w_m, S.w_q, S.w_k, S.w_s = (sb(f"s_w_{n}", [P, T, DIM]) for n in "mqks")
        S.b_m, S.b_s = sb("s_b_m", [P, DIM]), sb("s_b_s", [P, DIM])
        S.b_q, S.b_k = sb("s_b_q", [P, T]), sb("s_b_k", [P, T])

        W = Names()
        W.w, W.attn, W.r = A.e, A.pt, D.e
        W.a_w = D.pt[:, :, :, :].rearrange("p h t n -> p (h t n)").rearrange("p (t n) -> p t n", t=T)
        W.fc, W.g1, W.g2, W.g1_t = G.ha, G.hat, G.x_ha, G.pr
        W.map, W.q, W.k, W.gm, W.q_t, W.k_t = G.gt, G.df, G.pa, S.m, S.sq, S.u
        W.bw, W.ac, W.ab = sb("n_bw", [P, T, HG]), sb("n_ac", [P, T, HG]), sb("n_ab", [P, T, HG])
        W.mb, W.qb, W.kb, W.gb = (sb(f"n_{n}", [P, T]) for n in ("mb", "qb", "kb", "gb"))
        W.gb_rows = sb("n_gb_rows", [P, T, P])
        W.gcn, W.gcn_t = sb("n_gcn", [P, P]), sb("n_gcn_t", [P, P])
        w_loaded = ctx.enter_context(nc.semaphore("w_loaded"))
        gcn_zero = ctx.enter_context(nc.semaphore("gcn_zero"))
        const_ready = ctx.enter_context(nc.semaphore("const_ready"))
        w_psum = ctx.enter_context(nc.semaphore("w_psum"))
        w_sb = ctx.enter_context(nc.semaphore("w_sb"))

        def rows(ap):
            return ap.rearrange("(t p) n -> p t n", p=P)

        def column(ap):
            return ap.rearrange("(t p) -> p t", p=P)

        def spread(ap):
            return ap.rearrange("(a n) -> a n", a=1).broadcast_to([P, ap.shape[0]])

        loads = [(t[:, :, :], rows(d[n])) for t, n in (
            (A.wq, "L0_gnn_Wq"), (A.wk, "L0_gnn_Wk"), (A.wv, "L0_gnn_Wv"), (A.wo, "L0_gnn_Wo"),
            (D.wq, "L3_gnn_Wq"), (D.wk, "L3_gnn_Wk"), (D.wv, "L3_gnn_Wv"), (D.wo, "L3_gnn_Wo"),
            (W.a_w, "L1_gnn_A_w"), (W.fc, "L1_gnn_fc_w"), (W.g1, "L1_gnn_g1_w"), (W.g2, "L1_gnn_g2_w"),
            (W.map, "L2_gnn_map_w"), (W.q, "L2_gnn_q_w"), (W.k, "L2_gnn_k_w"), (W.gm, "L2_gnn_gcn_map_w"))]
        for h in range(HG):
            loads.append((W.w[:, h, :, :], rows(d["L1_gnn_W"][h])))
            loads.append((W.attn[:, h, :, :], rows(d["L1_gnn_attn"][h])))
            loads.append((W.bw[:, :, h], column(d["L1_gnn_bW"][h])))
        loads += [(t[:, :], column(d[n])) for t, n in (
            (W.mb, "L2_gnn_map_b"), (W.qb, "L2_gnn_q_b"), (W.kb, "L2_gnn_k_b"), (W.gb, "L2_gnn_gcn_map_b"))]
        loads += [(t[:, :], spread(ap)) for t, ap in (
            (A.bo, d["L0_gnn_bo"]), (D.bo, d["L3_gnn_bo"]), (S.b_m, d["L2_gnn_map_b"]), (G.b_gate, d["L1_gnn_gbias"]),
            (G.b_wh, d["L1_gnn_bW"].rearrange("h o -> (h o)")))]
        n_loads = len(loads) + P // DHS

        def transposed(src, dst_of):
            return (lambda pe, b: pe_transpose_rows(pe, b, src, C.ident), dst_of)

        block = ctx.enter_context(nc.Block())

        def pe_setup(pe):
            done = [0]

            def step(products, needs=0):
                n = done[0]
                if n >= 8:
                    needs = max(needs, n - 7)
                if needs:
                    pe.wait_ge(w_sb, needs)
                products(banks[n % 8]).then_inc(w_psum, 1)
                done[0] += 1
                return n + 1

            def mm_pairs(b, lhs, rhs_of, n=DIM):
                for mt in range(T):
                    for kc in range(T):
                        last = pe.matmul(b[:, mt * n:(mt + 1) * n], lhs[:, kc, mt * P:(mt + 1) * P], rhs_of(kc),
                                         start=(kc == 0), stop=(kc == T - 1))
                return last

            pe.wait_ge(w_loaded, 16 * n_loads)
            pe.wait_ge(const_ready, 5)
            for h in range(HG):
                step(lambda b: pe_transpose_rows(pe, b, W.w[:, h, :, :], C.ident))
            for cc in range(HG):
                step(lambda b: pe_transpose_rows(pe, b, W.a_w[:, :, cc * DIM:(cc + 1) * DIM], C.ident))
            for h in range(HG):
                r_done = step(lambda b: mm_pairs(b, W.attn[:, h, :, :], lambda kc: W.w[:, h, kc, :]))
            for h in range(HG):
                step(lambda b: mm_pairs(b, W.w[:, h, :, :], lambda kc: W.r[:, h, kc, :]), needs=r_done)
            for src in (W.fc, W.g2, W.g1, W.map, W.q, W.k):
                t_done = step(lambda b: pe_transpose_rows(pe, b, src, C.ident))
            step(lambda b: mm_pairs(b, W.fc, lambda kc: W.g1_t[:, kc, :]), needs=t_done)
            step(lambda b: mm_pairs(b, W.map, lambda kc: W.q_t[:, kc, :]))
            step(lambda b: mm_pairs(b, W.map, lambda kc: W.k_t[:, kc, :]))
            gcn_done = step(lambda b: pe.transpose(b[:, 0:P], W.gcn[:, :], C.ident[:, :]))

            def sem_weight(b):
                for kc in range(T):
                    for jt in range(T):
                        last = pe.matmul(b[:, kc * DIM + jt * P:kc * DIM + (jt + 1) * P],
                                         W.gm[:, jt, kc * P:(kc + 1) * P], W.gcn_t[:, :], start=True, stop=True)
                return last

            def sem_bias(b):
                for jt in range(T):
                    last = pe.matmul(b[:, jt * P:(jt + 1) * P], W.gb_rows[:, jt, :], W.gcn_t[:, :], start=True, stop=True)
                return last

            def columns(b, lhs_of, rhs_of, heads):
                for t in range(T):
                    for h in range(heads):
                        for kc in range(T):
                            last = pe.matmul(b[:, t * heads + h:t * heads + h + 1], lhs_of(h, kc, t), rhs_of(h, kc),
                                             start=(kc == 0), stop=(kc == T - 1))
                return last

            step(sem_weight, needs=gcn_done)
            step(sem_bias)
            step(lambda b: columns(b, lambda h, kc, t: W.q_t[:, kc, t * P:(t + 1) * P], lambda h, kc: W.mb[:, kc:kc + 1], 1))
            step(lambda b: columns(b, lambda h, kc, t: W.k_t[:, kc, t * P:(t + 1) * P], lambda h, kc: W.mb[:, kc:kc + 1], 1))
            step(lambda b: columns(b, lambda h, kc, t: W.r[:, h, kc, t * P:(t + 1) * P], lambda h, kc: W.bw[:, kc, h:h + 1], HG))
            a_done = step(lambda b: columns(b, lambda h, kc, t: W.attn[:, h, kc, t * P:(t + 1) * P],
                                            lambda h, kc: W.bw[:, kc, h:h + 1], HG))
            step(lambda b: columns(b, lambda h, kc, t: W.w[:, h, kc, t * P:(t + 1) * P],
                                   lambda h, kc: W.ac[:, kc, h:h + 1], HG), needs=a_done)

            def c_bias(b):
                for kc in range(T):
                    last = pe.matmul(b[:, 0:HG], C.ones[:, :], W.ab[:, kc, :], start=(kc == 0), stop=(kc == T - 1))
                return last

            step(c_bias, needs=a_done + 1)

        def dve_setup(dve):
            done = [0]

            def copy(dst, width=2 * DIM, inner=DIM, plus=None):
                n = done[0]
                dve.wait_ge(w_psum, n + 1)
                src = banks[n % 8][:, 0:width]
                if inner:
                    src = src.rearrange("p (a n) -> p a n", n=inner)
                if plus is None:
                    dve.tensor_copy(dst, src).then_inc(w_sb, 1)
                else:
                    dve.tensor_tensor(dst, src, plus, ALU.add).then_inc(w_sb, 1)
                done[0] += 1

            dve.wait_ge(w_loaded, 16 * n_loads)
            for jt in range(T):
                dve.tensor_scalar(W.gb_rows[:, jt, :], C.ones[:, :], W.gb[:, jt:jt + 1], None, ALU.mult)
            for h in range(HG):
                copy(G.w_t[:, :, h * DIM:(h + 1) * DIM])
            for cc in range(HG):
                copy(G.w_a[:, 2 * cc:2 * cc + 2, :])
            for h in range(HG):
                copy(W.r[:, h, :, :])
            for h in range(HG):
                copy(G.w_z[:, h, :, :])
            for dst in (G.w_fg[:, :, 0:DIM], G.w_g2[:, :, :], W.g1_t[:, :, :], S.w_m[:, :, :], W.q_t[:, :, :], W.k_t[:, :, :]):
                copy(dst)
            for dst in (G.w_fg[:, :, DIM:2 * DIM], S.w_q[:, :, :], S.w_k[:, :, :]):
                copy(dst)
            copy(W.gcn_t[:, :], P, None)
            copy(S.w_s[:, :, :])
            copy(S.b_s[:, :], DIM, None)
            copy(S.b_q[:, :], T, None, W.qb[:, :])
            copy(S.b_k[:, :], T, None, W.kb[:, :])
            copy(G.b_z[:, :, :], T * HG, HG)
            copy(W.ac[:, :, :], T * HG, HG)
            dve.wait_ge(w_sb, done[0])
            dve.tensor_tensor(W.ab[:, :, :], W.ac[:, :, :], W.bw[:, :, :], ALU.mult).then_inc(w_sb, 1)
            dve.wait_ge(w_psum, done[0] + 1)
            dve.tensor_copy(G.w_c[:, :, :], banks[done[0] % 8][:, 0:T * HG].rearrange("p (a n) -> p a n", n=HG)).then_inc(w_sb, 1)
            dve.wait_ge(w_psum, done[0] + 2)
            dve.tensor_copy(G.b_c[:, :], banks[(done[0] + 1) % 8][:, 0:HG]).then_inc(w_sb, 1)
            done[0] += 3
            return done[0]

        SETUP_COPIES = 4 * HG + 6 + 3 + 3 + 2 + 2 + 3

        def loop(eng, slot_a, slot_b):
            def body(a, b):
                for stage_a, stage_b in SCHEDULE:
                    if a is not None and stage_a:
                        slot_a(stage_a, a)
                    if b is not None and stage_b:
                        slot_b(stage_b, b)
            body(0, None)
            body(1, 0)
            with eng.Fori(2, GRAPHS) as t:
                body(t, t - 1)
            body(None, GRAPHS - 1)

        @block.sync
        def _(sp):
            sp.wait_ge(gcn_zero, 1)
            for n in range(P // DHS):
                sp.dma_start(W.gcn[n * DHS:(n + 1) * DHS, n * DHS:(n + 1) * DHS], d["L2_gnn_gcn_W"]).then_inc(w_loaded, 16)
            for dst, src in loads:
                sp.dma_start(dst, src, allow_slow_non_contiguous=True).then_inc(w_loaded, 16)

            def load_a(g):
                if later(g):
                    sp.wait_ge(A.x_bias.sem, A.x_bias.all(g - 1))
                if later(g):
                    sp.wait_ge(A.x_t_psum.sem, A.x_t_psum.all(g - 1))
                apart(sp)
                sp.dma_start(x_in[:, :, :], d["x"][g].rearrange("(t p) n -> p t n", p=P)).then_inc(x_loaded.sem, 16)
                if later(g):
                    sp.wait_ge(G.adj_bf_ready.sem, G.adj_bf_ready.all(g - 1))
                apart(sp)
                sp.dma_start(adj_a[:, :, :], d["adj"][g].rearrange("(t p) n -> p t n", p=P)).then_inc(adj_a_loaded.sem, 16)

            def load_b(g):
                if later(g):
                    sp.wait_ge(D.mask.sem, D.mask.all(g - 1))
                apart(sp)
                sp.dma_start(adj_b[:, :, :], d["adj"][g].rearrange("(t p) n -> p t n", p=P)).then_inc(adj_b_loaded.sem, 16)

            def store(g):
                sp.wait_ge(D.norm.out.sem, D.norm.out.at(g))
                apart(sp)
                sp.dma_start(out_dram[g].rearrange("(t p) n -> p t n", p=P), x4[:, :, :]).then_inc(stored.sem, 16)

            load_a(0)
            load_b(0)
            load_a(1)
            load_a(2)
            load_b(1)
            store(0)
            with sp.Fori(2, GRAPHS - 1) as t:
                load_a(t + 1)
                load_b(t)
                store(t - 1)
            load_b(GRAPHS - 1)
            store(GRAPHS - 2)
            store(GRAPHS - 1)
            sp.wait_ge(stored.sem, 16 * GRAPHS)

        @block.tensor
        def _(pe):
            pe_setup(pe)
            pe.wait_ge(w_sb, SETUP_COPIES)

            a_x_t, a_qkv, a_scores, a_probs, a_values, a_out = pe_attention(pe, A, C, x_in)
            d_x_t, d_qkv, d_scores, d_probs, d_values, d_out = pe_attention(pe, D, C, x3)

            def g_x_t(g):
                pe.wait_ge(G.adj_bf_ready.sem, G.adj_bf_ready.at(g))
                adj_bank = BA[3][:, 0:NODES].bitcast(BF16)
                for mt in range(T):
                    for nt in range(T):
                        last = pe.transpose(adj_bank[:, mt * NODES + nt * P:mt * NODES + (nt + 1) * P],
                                            G.adj_bf[:, nt, mt * P:(mt + 1) * P], C.ident_bf[:, :])
                last.then_inc(G.adj_psum.sem, 1)
                pe.wait_ge(A.norm.out.sem, A.norm.out.at(g))
                pe_transpose_rows(pe, BA[0], x1, C.ident).then_inc(G.x_t_psum.sem, 1)

            def g_wh(g):
                pe.wait_ge(G.adj_sb.sem, G.adj_sb.at(g))
                pe.wait_ge(G.x_t_sb.sem, G.x_t_sb.at(g))
                for n in range(4):
                    it, half = n // 2, n % 2
                    for kc in range(T):
                        last = pe.matmul(BA[(n + 1) % 4][:, :], G.xt[:, kc, it * P:(it + 1) * P],
                                         G.w_t[:, kc, half * BANK:(half + 1) * BANK], start=(kc == 0), stop=(kc == T - 1))
                    last.then_inc(G.wh_psum.sem, 1)

            def g_c(g):
                pe.wait_ge(G.wh_sb.sem, G.wh_sb.at(g, 2))
                for it in range(T):
                    for kc in range(T):
                        last = pe.matmul(BA[2][:, it * HG:(it + 1) * HG], G.xt[:, kc, it * P:(it + 1) * P],
                                         G.w_c[:, kc, :], start=(kc == 0), stop=(kc == T - 1))
                last.then_inc(G.c_psum.sem, 1)

            def g_z(g, h):
                if h < 2:
                    pe.wait_ge(G.wh_sb.sem, G.wh_sb.at(g, 4))
                else:
                    pe.wait_ge(G.z_sb.sem, G.z_sb.at(g, h - 1))
                pe_feature_major(pe, BA[h % 2], G.w_z[:, h, :, :], G.xt).then_inc(G.z_psum.sem, 1)

            def g_s(g, h):
                pe.wait_ge(G.z_sb.sem, G.z_sb.at(g, h + 1))
                if h == 0:
                    pe.wait_ge(G.c_sb.sem, G.c_sb.at(g))
                else:
                    pe.wait_ge(G.tanh.sem, G.tanh.at(g, h))
                for mt in range(T):
                    for kc in range(T):
                        last = pe.matmul(BA[2][:, mt * NODES:(mt + 1) * NODES], G.zt[:, h % 2, kc, mt * P:(mt + 1) * P],
                                         G.xt[:, kc, :], start=(kc == 0), stop=(kc == T - 1))
                last.then_inc(G.s_psum.sem, 1)

            def g_p(g, h):
                pe.wait_ge(G.a.sem, G.a.at(g, h + 1))
                if h in (1, 2):
                    pe.wait_ge(G.hp.sem, G.hp.at(g, h))
                bank = BA[3] if h < 3 else BA[0]
                if h == 0:
                    pe.wait_ge(G.wh_sb.sem, G.wh_sb.at(g, 4))
                if h == 3:
                    pe.wait_ge(G.z_sb.sem, G.z_sb.at(g, 4))
                for ot in range(T):
                    for mt in range(T):
                        last = pe.matmul(bank[:, ot * NODES:(ot + 1) * NODES],
                                         G.wh[:, mt, h * DIM + ot * P:h * DIM + (ot + 1) * P], G.am[:, h % 2, mt, :],
                                         start=(mt == 0), stop=(mt == T - 1))
                last.then_inc(G.p_psum.sem, 1)

            def g_ha(g):
                pe.wait_ge(G.hp.sem, G.hp.at(g, HG))
                for nt in range(T):
                    for n in range(HG * T):
                        last = pe.matmul(BA[1][:, nt * DIM:(nt + 1) * DIM], G.hpt[:, n // T, n % T, nt * P:(nt + 1) * P],
                                         G.w_a[:, n, :], start=(n == 0), stop=(n == HG * T - 1))
                last.then_inc(G.ha_psum.sem, 1)
                for nt in range(T):
                    for kc in range(T):
                        pe.matmul(BA[(3, 0)[nt]][:, :], G.xt[:, kc, nt * P:(nt + 1) * P], G.w_fg[:, kc, :],
                                  start=(kc == 0), stop=False)

            def g_ha_t(g):
                pe.wait_ge(G.ha_sb.sem, G.ha_sb.at(g))
                pe.wait_ge(G.tanh.sem, G.tanh.at(g, HG))
                pe_transpose_rows(pe, BA[2], G.ha, C.ident).then_inc(G.ha_t_psum.sem, 1)

            def g_gate(g):
                pe.wait_ge(G.ha_t_sb.sem, G.ha_t_sb.at(g))
                for nt in range(T):
                    for kc in range(T):
                        last = pe.matmul(BA[(3, 0)[nt]][:, DIM:2 * DIM], G.hat[:, kc, nt * P:(nt + 1) * P], G.w_g2[:, kc, :],
                                         start=False, stop=(kc == T - 1))
                    last.then_inc(G.gate_psum.sem, 1)

            def slot_a(stage, g):
                if stage == "a_x_t":
                    pe.wait_ge(x_loaded.sem, x_loaded.all(g))
                    if later(g):
                        pe.wait_ge(G.norm.sum.sem, G.norm.sum.all(g - 1))
                    a_x_t(g)
                elif stage == "a_qkv":
                    a_qkv(g)
                elif stage == "a_scores":
                    a_scores(g)
                elif stage == "a_probs_01":
                    a_probs(g, (0, 1))
                elif stage == "a_probs_23":
                    a_probs(g, (2, 3))
                elif stage == "a_values":
                    a_values(g)
                elif stage == "a_out":
                    a_out(g)
                elif stage == "g_x_t":
                    g_x_t(g)
                elif stage == "g_wh":
                    g_wh(g)
                    g_c(g)
                elif stage == "g_0":
                    g_z(g, 0)
                    g_z(g, 1)
                elif stage == "g_1":
                    g_s(g, 0)
                    g_z(g, 2)
                elif stage == "g_2":
                    g_s(g, 1)
                elif stage == "g_3":
                    g_p(g, 0)
                    g_z(g, 3)
                elif stage == "g_4":
                    g_s(g, 2)
                    g_p(g, 1)
                elif stage == "g_5":
                    g_s(g, 3)
                    g_p(g, 2)
                elif stage == "g_6":
                    g_p(g, 3)
                elif stage == "g_ha":
                    g_ha(g)
                elif stage == "g_ha_t":
                    g_ha_t(g)
                elif stage == "g_gate":
                    g_gate(g)

            def b_x_t(g):
                pe.wait_ge(G.norm.out.sem, G.norm.out.at(g))
                pe_transpose_rows(pe, BB[0], x2, C.ident).then_inc(S.x_t_psum.sem, 1)

            def b_project(g):
                pe.wait_ge(S.x_t_sb.sem, S.x_t_sb.at(g))
                if later(g):
                    pe.wait_ge(D.norm.sum.sem, D.norm.sum.all(g - 1))
                pe_node_major(pe, BB[1], S.xt, S.w_m).then_inc(S.m_psum.sem, 1)
                pe_feature_major(pe, BB[2], S.w_q, S.xt).then_inc(S.qk_psum.sem, 1)
                pe_feature_major(pe, BB[3], S.w_k, S.xt).then_inc(S.qk_psum.sem, 1)
                pe_node_major(pe, BB[0], S.xt, S.w_s).then_inc(S.sem_psum.sem, 1)

            def b_unit_t(g):
                pe.wait_ge(S.unit.sem, S.unit.at(g))
                pe_transpose_rows(pe, BB[1], S.u, C.ident).then_inc(S.unit_psum.sem, 1)

            def b_scores(g, h):
                if h == 0:
                    pe.wait_ge(S.mask.sem, S.mask.at(g))
                    pe.wait_ge(S.qk_sb.sem, S.qk_sb.at(g, 2))
                    pe.wait_ge(S.sem_sb.sem, S.sem_sb.at(g))
                elif h == 1:
                    pe.wait_ge(S.unit_sb.sem, S.unit_sb.at(g))
                else:
                    pe.wait_ge(S.exp.sem, S.exp.at(g, h - 1))
                rows = slice(DHS * (h % 4), DHS * (h % 4) + DHS)
                for it in range(T):
                    out = BB[h % 2][:, it * NODES:(it + 1) * NODES]
                    pe.matmul(out, C.ident_bf[:, :], S.add[:, it, :], start=True, stop=False)
                    last = pe.matmul(out, S.qt[rows, h // 4, it * P:(it + 1) * P], S.kt[rows, h // 4, :],
                                     start=False, stop=True)
                last.then_inc(S.s_psum.sem, 1)

            def b_cos(g, h):
                if h == 0:
                    pe.wait_ge(S.unit_sb.sem, S.unit_sb.at(g))
                    pe.wait_ge(S.qk_sb.sem, S.qk_sb.at(g, 2))
                else:
                    pe.wait_ge(S.cut.sem, S.cut.at(g, h))
                rows = slice(DHS * (h % 4), DHS * (h % 4) + DHS)
                for it in range(T):
                    last = pe.matmul(BB[2][:, it * NODES:(it + 1) * NODES], S.ut[rows, h // 4, it * P:(it + 1) * P],
                                     S.ut[rows, h // 4, :], start=True, stop=True)
                last.then_inc(S.cos_psum.sem, 1)

            def b_transpose(g, h):
                pe.wait_ge(S.a.sem, S.a.at(g, h + 1))
                if h == 4:
                    pe.wait_ge(S.o_sb.sem, S.o_sb.at(g, 1))
                elif h % 2:
                    pe.wait_ge(S.a_t_act.sem, S.a_t_act.at(g, (h + 1) // 2))
                elif h:
                    pe.wait_ge(S.a_t_dve.sem, S.a_t_dve.at(g, h // 2))
                for jt in range(T):
                    for it in range(T):
                        last = pe.transpose(BB[3][:, jt * NODES + it * P:jt * NODES + (it + 1) * P],
                                            S.cutp[:, h % 2, it, jt * P:(jt + 1) * P], C.ident[:, :])
                last.then_inc(S.a_t_psum.sem, 1)

            def b_values(g, half):
                pe.wait_ge(S.a_t_act.sem, S.a_t_act.at(g, 2 * half + 2))
                pe.wait_ge(S.a_t_dve.sem, S.a_t_dve.at(g, 2 * half + 2))
                for jt in range(T):
                    for n in range(4):
                        h = 4 * half + n
                        last = pe.matmul(BB[3][n * DHS:(n + 1) * DHS, 0:NODES], S.sem[:, jt, h * DHS:(h + 1) * DHS],
                                         S.at[:, n, jt, :], start=(jt == 0), stop=(jt == T - 1))
                last.then_inc(S.o_psum.sem, 1)

            def b_out(g):
                pe.wait_ge(S.o_sb.sem, S.o_sb.at(g, 2))
                pe_transpose_rows(pe, BB[0], S.ot, C.ident).then_inc(S.y_psum.sem, 1)

            def b_head(g, n):
                if n == 0:
                    b_scores(g, 0)
                    b_scores(g, 1)
                    b_cos(g, 0)
                else:
                    if n in (5, 9):
                        b_values(g, n // 8)
                    if n + 1 < HS:
                        b_scores(g, n + 1)
                    if n < HS:
                        b_cos(g, n)
                    if 0 <= n - 1 < HS:
                        b_transpose(g, n - 1)

            def slot_b(stage, g):
                if stage == "b_x_t":
                    b_x_t(g)
                elif stage == "b_project":
                    b_project(g)
                elif stage == "b_unit_t":
                    b_unit_t(g)
                elif stage.startswith("b_head"):
                    b_head(g, int(stage[7:]))
                elif stage == "b_out":
                    b_out(g)
                elif stage == "d_x_t":
                    pe.wait_ge(S.norm.out.sem, S.norm.out.at(g))
                    d_x_t(g)
                elif stage == "d_qkv":
                    d_qkv(g)
                elif stage == "d_scores":
                    d_scores(g)
                elif stage == "d_probs_01":
                    d_probs(g, (0, 1))
                elif stage == "d_probs_23":
                    d_probs(g, (2, 3))
                elif stage == "d_values":
                    d_values(g)
                elif stage == "d_out":
                    d_out(g)

            loop(pe, slot_a, slot_b)

        @block.scalar
        def _(act):
            act.wait_ge(w_sb, SETUP_COPIES)
            a_x_t, a_qkv, a_scores, a_probs, a_values = act_attention(act, A)
            d_x_t, d_qkv, d_scores, d_probs, d_values = act_attention(act, D)

            def g_z(g, h):
                act.wait_ge(G.z_psum.sem, G.z_psum.at(g, h + 1))
                for dt in range(T):
                    last = act.activation(G.zt[:, h % 2, dt, :], BA[h % 2][:, dt * NODES:(dt + 1) * NODES], ACT.Identity,
                                          bias=G.b_z[:, dt, h:h + 1])
                last.then_inc(G.z_sb.sem, 1)

            def g_s(g, h):
                act.wait_ge(G.s_psum.sem, G.s_psum.at(g, h + 1))
                if h == 0:
                    act.wait_ge(G.c_sb.sem, G.c_sb.at(g))
                if h >= 2:
                    act.wait_ge(G.a.sem, G.a.at(g, h - 1))
                else:
                    if later(g):
                        act.wait_ge(G.a.sem, G.a.at(g - 1, HG))
                for mt in range(T):
                    last = act.activation(G.th[:, h % 2, mt, :], BA[2][:, mt * NODES:(mt + 1) * NODES], ACT.Tanh,
                                          bias=G.c[:, mt, h:h + 1])
                last.then_inc(G.tanh.sem, 1)

            def slot_a(stage, g):
                if stage == "a_x_t":
                    a_x_t(g)
                elif stage == "a_qkv":
                    a_qkv(g)
                elif stage == "a_scores":
                    a_scores(g)
                elif stage == "a_probs_01":
                    a_probs(g, (0, 1))
                elif stage == "a_probs_23":
                    a_probs(g, (2, 3))
                elif stage == "a_values":
                    a_values(g)
                elif stage == "g_x_t":
                    act.wait_ge(G.x_t_psum.sem, G.x_t_psum.at(g))
                    act.activation(G.xt[:, :, :], view(BA[0]), ACT.Copy).then_inc(G.x_t_sb.sem, 1)
                elif stage == "g_0":
                    g_z(g, 0)
                    g_z(g, 1)
                elif stage == "g_1":
                    g_s(g, 0)
                    g_z(g, 2)
                elif stage == "g_2":
                    g_s(g, 1)
                elif stage == "g_3":
                    g_z(g, 3)
                elif stage == "g_4":
                    g_s(g, 2)
                elif stage == "g_5":
                    g_s(g, 3)
                elif stage == "g_ha":
                    act.wait_ge(G.ha_psum.sem, G.ha_psum.at(g))
                    if later(g):
                        act.wait_ge(G.diff.sem, G.diff.all(g - 1))
                    if later(g):
                        act.wait_ge(G.x_ha_done.sem, G.x_ha_done.all(g - 1))
                    act.activation(G.ha[:, :, :], view(BA[1]), ACT.Copy).then_inc(G.ha_sb.sem, 1)
                elif stage == "g_gate":
                    for nt in range(T):
                        if later(g):
                            act.wait_ge(G.part.sem, G.part.all(g - 1))
                        act.wait_ge(G.pre.sem, G.pre.at(g, nt + 1))
                        act.activation(G.gt[:, nt, :], G.pr[:, nt, :], ACT.Tanh, scale=0.5).then_inc(G.gate.sem, 1)

            def exps(g, h):
                act.wait_ge(S.shift.sem, S.shift.at(g, h + 1))
                if h >= 2:
                    act.wait_ge(S.cut.sem, S.cut.at(g, h - 1))
                else:
                    if later(g):
                        act.wait_ge(S.cut.sem, S.cut.all(g - 1))
                for it in range(T):
                    last = act.activation(S.e[:, h % 2, it, :], BB[h % 2][:, it * NODES:(it + 1) * NODES], ACT.Exp,
                                          bias=S.sh[:, h, it:it + 1], scale=DHS ** -0.5, accum_out=S.sums[:, h, it:it + 1])
                last.then_inc(S.exp.sem, 1)

            def copy_t(g, h):
                if h % 2 == 0:
                    act.wait_ge(S.a_t_psum.sem, S.a_t_psum.at(g, h + 1))
                    act.activation(S.at[:, h % 4, :, :], view(BB[3]), ACT.Copy).then_inc(S.a_t_act.sem, 1)

            def relu(g, half):
                act.wait_ge(S.o_psum.sem, S.o_psum.at(g, half + 1))
                act.activation(S.ot[:, half, :], BB[3][:, 0:NODES], ACT.Relu).then_inc(S.o_sb.sem, 1)

            def slot_b(stage, g):
                if stage == "b_x_t":
                    act.wait_ge(S.x_t_psum.sem, S.x_t_psum.at(g))
                    act.activation(S.xt[:, :, :], view(BB[0]), ACT.Copy).then_inc(S.x_t_sb.sem, 1)
                elif stage == "b_project":
                    for n, (dst, bias) in enumerate(((S.qt, S.b_q), (S.kt, S.b_k))):
                        act.wait_ge(S.qk_psum.sem, S.qk_psum.at(g, n + 1))
                        for jt in range(T):
                            last = act.activation(dst[:, jt, :], BB[2 + n][:, jt * NODES:(jt + 1) * NODES], ACT.Identity,
                                                  bias=bias[:, jt:jt + 1])
                        last.then_inc(S.qk_sb.sem, 1)
                elif stage == "b_unit_t":
                    act.wait_ge(S.unit_psum.sem, S.unit_psum.at(g))
                    act.activation(S.ut[:, :, :], view(BB[1]), ACT.Copy).then_inc(S.unit_sb.sem, 1)
                elif stage.startswith("b_head"):
                    n = int(stage[7:])
                    if n in (5, 9):
                        relu(g, n // 8)
                    if n == 0:
                        exps(g, 0)
                    if 1 <= n and n - 1 < HS:
                        if n < HS:
                            exps(g, n)
                        copy_t(g, n - 1)
                elif stage == "d_x_t":
                    d_x_t(g)
                elif stage == "d_qkv":
                    d_qkv(g)
                elif stage == "d_scores":
                    d_scores(g)
                elif stage == "d_probs_01":
                    d_probs(g, (0, 1))
                elif stage == "d_probs_23":
                    d_probs(g, (2, 3))
                elif stage == "d_values":
                    d_values(g)

            loop(act, slot_a, slot_b)

        @block.vector
        def _(dve):
            dve.wait_ge(const_ready, 5)
            copies = dve_setup(dve)
            assert copies == SETUP_COPIES, copies
            dve.wait_ge(w_sb, SETUP_COPIES)
            a_qkv, a_scores, a_probs, a_finish = dve_attention(dve, A)
            d_qkv, d_scores, d_probs, d_finish = dve_attention(dve, D)

            def g_hp(g, h):
                dve.wait_ge(G.p_psum.sem, G.p_psum.at(g, h + 1))
                if h == 0:
                    if later(g):
                        dve.wait_ge(G.ha_psum.sem, G.ha_psum.all(g - 1))
                bank = BA[3] if h < 3 else BA[0]
                dve.tensor_scalar(G.hpt[:, h, :, :], view(bank), 0.0, None, ALU.max).then_inc(G.hp.sem, 1)

            def slot_a(stage, g):
                if stage == "a_qkv":
                    a_qkv(g)
                elif stage == "a_scores":
                    a_scores(g)
                elif stage == "a_probs_01":
                    a_probs(g, (0, 1))
                elif stage == "a_probs_23":
                    a_probs(g, (2, 3))
                elif stage == "a_out":
                    a_finish(g)
                    if later(g):
                        dve.wait_ge(G.x_t_psum.sem, G.x_t_psum.all(g - 1))
                        dve.wait_ge(G.x_ha_done.sem, G.x_ha_done.all(g - 1))
                    dve_norm_out(dve, A.norm, g, x1)
                elif stage == "g_x_t":
                    dve.wait_ge(G.adj_psum.sem, G.adj_psum.at(g))
                    if later(g):
                        dve.wait_ge(G.a.sem, G.a.all(g - 1))
                    dve.tensor_copy(G.adj_t[:, :, :], BA[3][:, 0:NODES].bitcast(BF16).rearrange("p (a n) -> p a n", n=NODES))\
                        .then_inc(G.adj_sb.sem, 1)
                elif stage == "g_wh":
                    if later(g):
                        dve.wait_ge(G.p_psum.sem, G.p_psum.all(g - 1))
                    for n in range(4):
                        it, half = n // 2, n % 2
                        cols = slice(half * BANK, (half + 1) * BANK)
                        dve.wait_ge(G.wh_psum.sem, G.wh_psum.at(g, n + 1))
                        dve.tensor_tensor(G.wh[:, it, cols], BA[(n + 1) % 4][:, :], G.b_wh[:, cols], ALU.add)\
                            .then_inc(G.wh_sb.sem, 1)
                    dve.wait_ge(G.c_psum.sem, G.c_psum.at(g))
                    if later(g):
                        dve.wait_ge(G.tanh.sem, G.tanh.all(g - 1))
                    for it in range(T):
                        last = dve.tensor_tensor(G.c[:, it, :], BA[2][:, it * HG:(it + 1) * HG], G.b_c[:, :], ALU.add)
                    last.then_inc(G.c_sb.sem, 1)
                elif stage == "g_3":
                    g_hp(g, 0)
                elif stage == "g_4":
                    g_hp(g, 1)
                elif stage == "g_5":
                    g_hp(g, 2)
                elif stage == "g_6":
                    g_hp(g, 3)
                elif stage == "g_ha_t":
                    dve.wait_ge(G.ha_t_psum.sem, G.ha_t_psum.at(g))
                    dve.tensor_copy(G.hat[:, :, :], view(BA[2])).then_inc(G.ha_t_sb.sem, 1)
                elif stage == "g_gate":
                    for nt in range(T):
                        bank = BA[(3, 0)[nt]]
                        dve.wait_ge(G.gate_psum.sem, G.gate_psum.at(g, nt + 1))
                        if later(g):
                            dve.wait_ge(G.gate.sem, G.gate.all(g - 1))
                        dve.tensor_tensor(G.pr[:, nt, :], bank[:, DIM:2 * DIM], G.b_gate[:, :], ALU.add).then_inc(G.pre.sem, 1)
                        dve.wait_ge(G.ha_sb.sem, G.ha_sb.at(g))
                        dve.tensor_tensor(G.df[:, nt, :], bank[:, 0:DIM], G.ha[:, nt, :], ALU.subtract).then_inc(G.diff.sem, 1)
                    dve.wait_ge(G.x_ha_done.sem, G.x_ha_done.at(g))
                    for nt in range(T):
                        dve.wait_ge(G.diff.sem, G.diff.at(g, nt + 1))
                        dve.wait_ge(G.gate.sem, G.gate.at(g, nt + 1))
                        dve.scalar_tensor_tensor(G.pa[:, nt, :], G.gt[:, nt, :], 1.0, G.df[:, nt, :], ALU.add, ALU.mult)\
                            .then_inc(G.part.sem, 1)
                    dve.wait_ge(G.part.sem, G.part.at(g, T))
                    dve.scalar_tensor_tensor(G.norm.r[:, :, :], G.pa[:, :, :], 0.5, G.x_ha[:, :, :], ALU.mult, ALU.add)\
                        .then_inc(G.norm.sum.sem, 1)
                    dve_norm_stats(dve, G.norm, g)
                    if later(g):
                        dve.wait_ge(S.x_t_psum.sem, S.x_t_psum.all(g - 1))
                        dve.wait_ge(S.norm.sum.sem, S.norm.sum.all(g - 1))
                    dve_norm_out(dve, G.norm, g, x2)

            def cut(g, h):
                dve.wait_ge(S.cos_psum.sem, S.cos_psum.at(g, h + 1))
                dve.wait_ge(S.exp.sem, S.exp.at(g, h + 1))
                if h >= 2:
                    dve.wait_ge(S.a_t_psum.sem, S.a_t_psum.at(g, h - 1))
                else:
                    if later(g):
                        dve.wait_ge(S.a_t_psum.sem, S.a_t_psum.all(g - 1))
                for it in range(T):
                    last = dve.scalar_tensor_tensor(S.cutp[:, h % 2, it, :], BB[2][:, it * NODES:(it + 1) * NODES], COS_MIN,
                                                    S.e[:, h % 2, it, :], ALU.is_gt, ALU.mult, accum_out=S.dsum[:, h, it:it + 1])
                last.then_inc(S.cut.sem, 1)

            def maxima(g, h):
                dve.wait_ge(S.s_psum.sem, S.s_psum.at(g, h + 1))
                if h == 0:
                    if later(g):
                        dve.wait_ge(S.shift.sem, S.shift.all(g - 1))
                dve.reduce_max(S.mx[:, h, :], view(BB[h % 2]), AX_X).then_inc(S.max.sem, 1)

            def copy_t(g, h):
                if h % 2 == 1:
                    dve.wait_ge(S.a_t_psum.sem, S.a_t_psum.at(g, h + 1))
                    dve.tensor_copy(S.at[:, h % 4, :, :], view(BB[3])).then_inc(S.a_t_dve.sem, 1)

            def slot_b(stage, g):
                if stage == "b_project":
                    dve.wait_ge(S.m_psum.sem, S.m_psum.at(g))
                    if later(g):
                        dve.wait_ge(S.unit.sem, S.unit.all(g - 1))
                    for it in range(T):
                        last = dve.tensor_tensor(S.m[:, it, :], BB[1][:, it * DIM:(it + 1) * DIM], S.b_m[:, :], ALU.add)
                    last.then_inc(S.m_sb.sem, 1)
                    dve.wait_ge(S.sem_psum.sem, S.sem_psum.at(g))
                    if later(g):
                        dve.wait_ge(S.o_psum.sem, S.o_psum.all(g - 1))
                    for it in range(T):
                        last = dve.tensor_tensor(S.sem[:, it, :], BB[0][:, it * DIM:(it + 1) * DIM], S.b_s[:, :], ALU.add)
                    last.then_inc(S.sem_sb.sem, 1)
                    dve.wait_ge(S.square.sem, S.square.at(g))
                    dve.reduce_sum(S.ss[:, :], S.sq[:, :, :].rearrange("p t (h n) -> p (t h) n", n=DHS), AX_X)\
                        .then_inc(S.sumsq.sem, 1)
                elif stage.startswith("b_head"):
                    n = int(stage[7:])
                    if n == 0:
                        maxima(g, 0)
                        maxima(g, 1)
                        cut(g, 0)
                    else:
                        if n + 1 < HS:
                            maxima(g, n + 1)
                        if n < HS:
                            cut(g, n)
                        if n - 1 < HS:
                            copy_t(g, n - 1)
                elif stage == "b_out":
                    dve.wait_ge(S.y_psum.sem, S.y_psum.at(g))
                    dve.tensor_tensor(S.norm.r[:, :, :], view(BB[0]), x2[:, :, :], ALU.add).then_inc(S.norm.sum.sem, 1)
                    dve_norm_stats(dve, S.norm, g)
                    if later(g):
                        dve.wait_ge(D.x_t_psum.sem, D.x_t_psum.all(g - 1))
                        dve.wait_ge(D.x_bias.sem, D.x_bias.all(g - 1))
                    dve_norm_out(dve, S.norm, g, x3)
                elif stage == "d_qkv":
                    d_qkv(g)
                elif stage == "d_scores":
                    d_scores(g)
                elif stage == "d_probs_01":
                    d_probs(g, (0, 1))
                elif stage == "d_probs_23":
                    d_probs(g, (2, 3))
                elif stage == "d_out":
                    d_finish(g)
                    if later(g):
                        dve.wait_ge(stored.sem, stored.all(g - 1))
                    dve_norm_out(dve, D.norm, g, x4)

            loop(dve, slot_a, slot_b)

        @block.gpsimd
        def _(pool):
            pool.memset(W.gcn[:, :], 0.0).then_inc(gcn_zero, 1)
            pool.memset(C.ident[:, :], 0.0).then_inc(const_ready, 1)
            pool.memset(C.minus_one[:, :], -1.0)
            pool.memset(C.minus_half[:, :], -0.5).then_inc(const_ready, 1)
            pool.memset(C.ones[:, :], 1.0).then_inc(const_ready, 1)
            pool.wait_ge(const_ready, 3)
            pool.affine_select(out=C.ident[:, :], in_=C.ident[:, :], compare_op=ALU.not_equal, fill=1.0, base=0,
                               pattern=[[-1, P]], channel_multiplier=1).then_inc(const_ready, 1)
            pool.wait_ge(const_ready, 4)
            pool.tensor_copy(C.ident_bf[:, :], C.ident[:, :]).then_inc(const_ready, 1)
            pool.wait_ge(w_loaded, 16 * n_loads)
            pool.wait_ge(w_sb, SETUP_COPIES)
            a_scores, a_normalise, a_finish = pool_attention(pool, A, C)
            d_scores, d_normalise, d_finish = pool_attention(pool, D, C)

            def g_a(g, h):
                pool.wait_ge(G.tanh.sem, G.tanh.at(g, h + 1))
                if h == 0:
                    pool.wait_ge(G.adj_sb.sem, G.adj_sb.at(g))
                if h >= 2:
                    pool.wait_ge(G.p_psum.sem, G.p_psum.at(g, h - 1))
                else:
                    if later(g):
                        pool.wait_ge(G.p_psum.sem, G.p_psum.all(g - 1))
                pool.tensor_tensor(G.am[:, h % 2, :, :], G.th[:, h % 2, :, :], G.adj_t[:, :, :], ALU.mult)\
                    .then_inc(G.a.sem, 1)

            def slot_a(stage, g):
                if stage == "a_x_t":
                    pool.wait_ge(x_loaded.sem, x_loaded.all(g))
                    pool.wait_ge(adj_a_loaded.sem, adj_a_loaded.all(g))
                    pool_attention_inputs(pool, A, g, x_in, adj_a)
                    if later(g):
                        pool.wait_ge(G.adj_psum.sem, G.adj_psum.all(g - 1))
                    apart(pool)
                    pool.tensor_copy(G.adj_bf[:, :, :], adj_a[:, :, :]).then_inc(G.adj_bf_ready.sem, 1)
                elif stage == "a_scores":
                    a_scores(g)
                    a_normalise(g)
                elif stage == "a_out":
                    a_finish(g)
                elif stage == "g_1":
                    g_a(g, 0)
                elif stage == "g_2":
                    g_a(g, 1)
                elif stage == "g_4":
                    g_a(g, 2)
                elif stage == "g_5":
                    g_a(g, 3)
                elif stage == "g_ha":
                    pool.wait_ge(G.ha_sb.sem, G.ha_sb.at(g))
                    pool.wait_ge(A.norm.out.sem, A.norm.out.at(g))
                    if later(g):
                        pool.wait_ge(G.norm.sum.sem, G.norm.sum.all(g - 1))
                    pool.tensor_tensor(G.x_ha[:, :, :], G.ha[:, :, :], x1[:, :, :], ALU.add).then_inc(G.x_ha_done.sem, 1)
                elif stage == "g_gate":
                    pool_norm(pool, G.norm, C, g)

            def shift(g, h):
                pool.wait_ge(S.max.sem, S.max.at(g, h + 1))
                if h == 0:
                    if later(g):
                        pool.wait_ge(S.exp.sem, S.exp.all(g - 1))
                apart(pool)
                pool.tensor_scalar(S.sh[:, h, :], S.mx[:, h, :], MAX_FLOOR, -(DHS ** -0.5), ALU.max, ALU.mult).then_inc(S.shift.sem, 1)

            def normalise(g, h):
                pool.wait_ge(S.cut.sem, S.cut.at(g, h + 1))
                pool.tensor_tensor(S.f1[:, h, :], S.dsum[:, h, :], S.sums[:, h, :], ALU.add).then_inc(S.f[0].sem, 1)
                pool.wait_ge(S.f[0].sem, S.f[0].at(g, h + 1))
                pool.tensor_tensor(S.f2[:, h, :], S.f1[:, h, :], S.drop[:, :], ALU.add).then_inc(S.f[1].sem, 1)
                pool.wait_ge(S.f[1].sem, S.f[1].at(g, h + 1))
                pool.tensor_tensor(S.f3[:, h, :], S.f2[:, h, :], C.minus_one[:, 0:T], ALU.pow).then_inc(S.f[2].sem, 1)
                pool.wait_ge(S.f[2].sem, S.f[2].at(g, h + 1))
                pool.tensor_tensor(S.fac[:, h, :], S.f3[:, h, :], S.kp[:, :], ALU.mult).then_inc(S.f[3].sem, 1)
                pool.wait_ge(S.f[3].sem, S.f[3].at(g, h + 1))
                apart(pool)
                for it in range(T):
                    last = pool.tensor_scalar(S.cutp[:, h % 2, it, :], S.cutp[:, h % 2, it, :], S.fac[:, h, it:it + 1],
                                              None, ALU.mult)
                last.then_inc(S.a.sem, 1)

            def slot_b(stage, g):
                if stage == "b_x_t":
                    pool.wait_ge(adj_b_loaded.sem, adj_b_loaded.at(g, 16))
                    if later(g):
                        pool.wait_ge(S.s_psum.sem, S.s_psum.all(g - 1))
                    apart(pool)
                    pool.tensor_scalar(S.add[:, :, :], adj_b[:, :, :], MASKED, None, ALU.mult).then_inc(S.mask.sem, 1)
                    if later(g):
                        pool.wait_ge(S.a.sem, S.a.all(g - 1))
                    apart(pool)
                    pool.tensor_copy(S.drop[:, :], adj_b[:, :, 0])
                    pool.tensor_scalar(S.kp[:, :], adj_b[:, :, 0], -1.0, 1.0, ALU.mult, ALU.add).then_inc(S.keep.sem, 1)
                elif stage == "b_project":
                    pool.wait_ge(S.m_sb.sem, S.m_sb.at(g))
                    pool.tensor_tensor(S.sq[:, :, :], S.m[:, :, :], S.m[:, :, :], ALU.mult).then_inc(S.square.sem, 1)
                    pool.wait_ge(S.sumsq.sem, S.sumsq.at(g))
                    apart(pool)
                    pool.tensor_scalar(S.fl[:, :], S.ss[:, :], COS_EPS * COS_EPS, None, ALU.max).then_inc(S.floor.sem, 1)
                    pool.wait_ge(S.floor.sem, S.floor.at(g))
                    pool.tensor_tensor(S.inv[:, :], S.fl[:, :], C.minus_half[:, :], ALU.pow).then_inc(S.inorm.sem, 1)
                    pool.wait_ge(S.inorm.sem, S.inorm.at(g))
                    if later(g):
                        pool.wait_ge(S.unit_psum.sem, S.unit_psum.all(g - 1))
                    pool.tensor_tensor(S.u[:, :, :].rearrange("p t (h n) -> p (t h) n", n=DHS),
                                       S.m[:, :, :].rearrange("p t (h n) -> p (t h) n", n=DHS),
                                       S.inv[:, :].rearrange("p (h a) -> p h a", a=1).broadcast_to([P, T * HS, DHS]),
                                       ALU.mult).then_inc(S.unit.sem, 1)
                    pool.wait_ge(S.keep.sem, S.keep.at(g))
                elif stage.startswith("b_head"):
                    n = int(stage[7:])
                    if n == 0:
                        shift(g, 0)
                        shift(g, 1)
                        normalise(g, 0)
                    else:
                        if n + 1 < HS:
                            shift(g, n + 1)
                        if n < HS:
                            normalise(g, n)
                elif stage == "b_out":
                    pool_norm(pool, S.norm, C, g)
                elif stage == "d_x_t":
                    pool.wait_ge(S.norm.out.sem, S.norm.out.at(g))
                    pool_attention_inputs(pool, D, g, x3, adj_b)
                elif stage == "d_scores":
                    d_scores(g)
                    d_normalise(g)
                elif stage == "d_out":
                    d_finish(g)

            loop(pool, slot_a, slot_b)


INPUTS = ["x", "adj", "L0_gnn_Wq", "L0_gnn_Wk", "L0_gnn_Wv", "L0_gnn_Wo", "L0_gnn_bo", "L1_gnn_W", "L1_gnn_bW", "L1_gnn_attn",
          "L1_gnn_A_w", "L1_gnn_fc_w", "L1_gnn_g1_w", "L1_gnn_g2_w", "L1_gnn_gbias", "L2_gnn_map_w", "L2_gnn_map_b",
          "L2_gnn_q_w", "L2_gnn_q_b", "L2_gnn_k_w", "L2_gnn_k_b", "L2_gnn_gcn_map_w", "L2_gnn_gcn_map_b", "L2_gnn_gcn_W",
          "L3_gnn_Wq", "L3_gnn_Wk", "L3_gnn_Wv", "L3_gnn_Wo", "L3_gnn_bo"]


def kernel(**inputs):
    import concourse.bacc as bacc
    from concourse.bass_utils import run_bass_kernel_spmd

    nc = bacc.Bacc("TRN2", target_bir_lowering=False, num_devices=1)
    arrays, dram = {}, {}
    for name in INPUTS:
        a = np.ascontiguousarray(inputs[name])
        arrays[f"in_{name}"] = a
        dram[name] = nc.dram_tensor(f"in_{name}", a.shape, mybir.dt.from_np(a.dtype), kind="ExternalInput").ap()
    out = nc.dram_tensor("out", (GRAPHS, NODES, DIM), F32, kind="ExternalOutput").ap()
    build(nc, dram, out)
    result = run_bass_kernel_spmd(nc, [arrays], core_ids=[0])
    return result.results[0]["out"]
```

```python
from contextlib import ExitStack

import numpy as np
import concourse.bass as bass
import concourse.mybir as mybir
from concourse.alu_op_type import AluOpType as ALU

ACT = mybir.ActivationFunctionType
AX_X = mybir.AxisListType.X
F32 = mybir.dt.float32
F32R = mybir.dt.float32r
BF16 = mybir.dt.bfloat16
U8 = mybir.dt.uint8

GRAPHS, NODES, DIM = 32, 256, 256
P = 128
T = NODES // P
HA, DHA = 4, 64
HG = 4
HS, DHS = 8, 32
COS_MIN = 0.1
COS_EPS = 1e-8
LN_EPS = 1e-5
MASKED = -3.3e38
MAX_FLOOR = -1e30
BANK = 512

SCHEDULE = [
    ("a_inputs", 0), ("a_x_t", 0), ("d_scores", 2), ("g_mix", 1), ("a_qkv", 0), ("g_norm_out", 1),
    ("d_norm", 2), ("a_scores", 0), ("d_probs_01", 2), ("d_probs_23", 2), ("a_exps", 0),
    ("d_values", 2), ("b_x_t", 1), ("a_norm", 0), ("d_out", 2), ("a_probs_01", 0), ("a_probs_23", 0),
    ("b_project", 1), ("a_values", 0), ("b_unit_t", 1), ("d_norm_out", 2),
    ("b_head_0", 1), ("b_scale_0", 1), ("a_out", 0),
    ("b_head_1", 1), ("b_scale_1", 1),
    ("b_head_2", 1), ("b_scale_2", 1), ("a_sum", 0),
    ("b_head_3", 1), ("a_norm_out", 0), ("b_scale_3", 1), ("g_x_t", 0),
    ("b_head_4", 1), ("b_scale_4", 1), ("g_0", 0),
    ("b_head_5", 1), ("b_scale_5", 1), ("g_1", 0),
    ("b_head_6", 1), ("g_p_0", 0), ("b_scale_6", 1), ("g_2", 0),
    ("b_head_7", 1), ("g_p_1", 0), ("b_scale_7", 1), ("g_3", 0),
    ("b_head_8", 1), ("g_p_2", 0), ("g_4", 0), ("b_head_9", 1), ("g_ha_0", 0), ("b_out", 1), ("g_p_3", 0),
    ("b_norm_out", 1), ("g_ha_1", 0), ("d_x_t", 1), ("g_ha_t", 0), ("d_qkv", 1), ("g_gate", 0),
]
LAG = 2


class Signal:

    def __init__(self, ctx, nc, name, per=1):
        self.sem = ctx.enter_context(nc.semaphore(name))
        self.per = per

    def at(self, g, k=1):
        return g * self.per + k

    def all(self, g):
        return g * self.per + self.per


def apart(eng):
    eng.nop(nofuse=True)


def later(g):
    return not isinstance(g, int) or g > 0


class Names:
    pass


def norm_signals(ctx, nc, name):
    N = Names()
    N.sum = Signal(ctx, nc, f"{name}_sum")
    N.stats = Signal(ctx, nc, f"{name}_stats")
    N.var = Signal(ctx, nc, f"{name}_var")
    N.eps = Signal(ctx, nc, f"{name}_eps")
    N.rstd = Signal(ctx, nc, f"{name}_rstd")
    N.out = Signal(ctx, nc, f"{name}_out")
    return N


def norm_buffers(ctx, nc, N, name, rows):
    N.r = rows
    N.st = ctx.enter_context(nc.sbuf_tensor(f"{name}_st", [P, T, 6], F32))
    N.mv = ctx.enter_context(nc.sbuf_tensor(f"{name}_mv", [P, T, 2], F32))
    N.ve = ctx.enter_context(nc.sbuf_tensor(f"{name}_ve", [P, T], F32))
    N.rs = ctx.enter_context(nc.sbuf_tensor(f"{name}_rs", [P, T], F32))


def dve_norm_stats(dve, N, g):
    dve.wait_ge(N.sum.sem, N.sum.at(g))
    for it in range(T):
        last = dve.bn_stats(N.st[:, it, :], N.r[:, it, :])
    last.then_inc(N.stats.sem, 1)
    dve.wait_ge(N.stats.sem, N.stats.at(g))
    apart(dve)
    for it in range(T):
        last = dve.bn_aggr(N.mv[:, it, :], N.st[:, it, :])
    last.then_inc(N.var.sem, 1)


def dve_norm_out(dve, N, g):
    dve.wait_ge(N.rstd.sem, N.rstd.at(g))
    for it in range(T):
        last = dve.tensor_scalar(N.r[:, it, :], N.r[:, it, :], N.mv[:, it, 0:1], N.rs[:, it:it + 1],
                                 ALU.subtract, ALU.mult)
    last.then_inc(N.out.sem, 1)


def pool_norm(pool, N, C, g):
    pool.wait_ge(N.var.sem, N.var.at(g))
    apart(pool)
    pool.tensor_scalar(N.ve[:, :], N.mv[:, :, 1], LN_EPS, None, ALU.add).then_inc(N.eps.sem, 1)
    pool.wait_ge(N.eps.sem, N.eps.at(g))
    pool.tensor_tensor(N.rs[:, :], N.ve[:, :], C.minus_half[:, 0:T], ALU.pow).then_inc(N.rstd.sem, 1)


def attention_layer(ctx, nc, name, banks, rows, split):
    L = Names()
    L.banks = banks
    L.split = split
    L.x_t_psum = Signal(ctx, nc, f"{name}_x_t_psum")
    L.x_t_hi = Signal(ctx, nc, f"{name}_x_t_hi")
    L.x_t_sb = Signal(ctx, nc, f"{name}_x_t_sb")
    L.qkv_psum = Signal(ctx, nc, f"{name}_qkv_psum", 3)
    L.qk_sb = Signal(ctx, nc, f"{name}_qk_sb", 2)
    L.v_sb = Signal(ctx, nc, f"{name}_v_sb")
    L.s_psum = Signal(ctx, nc, f"{name}_s_psum", HA)
    L.max = Signal(ctx, nc, f"{name}_max", HA)
    L.shift = Signal(ctx, nc, f"{name}_shift", HA)
    L.exp = Signal(ctx, nc, f"{name}_exp", HA)
    L.inv = Signal(ctx, nc, f"{name}_inv", HA)
    L.p = Signal(ctx, nc, f"{name}_p", HA)
    L.p_t_psum = Signal(ctx, nc, f"{name}_p_t_psum", HA)
    L.p_t_act = Signal(ctx, nc, f"{name}_p_t_act", HA // 2)
    L.p_t_dve = Signal(ctx, nc, f"{name}_p_t_dve", HA // 2)
    L.o_psum = Signal(ctx, nc, f"{name}_o_psum")
    L.o_hi = Signal(ctx, nc, f"{name}_o_hi")
    L.o_sb = Signal(ctx, nc, f"{name}_o_sb")
    L.y_psum = Signal(ctx, nc, f"{name}_y_psum")
    L.x_bias = Signal(ctx, nc, f"{name}_x_bias")
    L.mask = Signal(ctx, nc, f"{name}_mask")
    L.norm = norm_signals(ctx, nc, name)

    def sb(what, shape, dt=F32):
        return ctx.enter_context(nc.sbuf_tensor(f"{name}_{what}", shape, dt))

    L.mx = sb("mx", [P, HA, T])
    L.sh = sb("sh", [P, HA, T])
    L.sums = sb("sums", [P, HA, T])
    L.iv = sb("iv", [P, HA, T])
    L.add = sb("add", [P, T, NODES], BF16)
    L.bo = sb("bo", [P, DIM])
    norm_buffers(ctx, nc, L.norm, name, rows)
    return L


def view(bank, inner=NODES):
    return bank[:, :].rearrange("p (a n) -> p a n", n=inner)


def pe_transpose_rows(pe, out_bank, rows, ident):
    for kc in range(T):
        for it in range(T):
            last = pe.transpose(out_bank[:, kc * NODES + it * P:kc * NODES + (it + 1) * P],
                                rows[:, it, kc * P:(kc + 1) * P], ident[:, :])
    return last


def pe_product(pe, out, w, x, first, last):
    if not isinstance(w, tuple):
        return pe.matmul(out, w, x, start=first, stop=last)
    pe.matmul(out, w[0], x[0], start=first, stop=False)
    pe.matmul(out, w[0], x[1], start=False, stop=False)
    return pe.matmul(out, w[1], x[0], start=False, stop=last)


def part(t, *at):
    return tuple(half[at] for half in t) if isinstance(t, tuple) else t[at]


def pe_feature_major(pe, out_bank, w, x_t):
    for jt in range(T):
        for kc in range(T):
            last = pe_product(pe, out_bank[:, jt * NODES:(jt + 1) * NODES],
                              part(w, slice(None), kc, slice(jt * P, (jt + 1) * P)), part(x_t, slice(None), kc),
                              kc == 0, kc == T - 1)
    return last


def pe_node_major(pe, out_bank, x_t, w):
    for it in range(T):
        for kc in range(T):
            last = pe_product(pe, out_bank[:, it * DIM:(it + 1) * DIM],
                              part(x_t, slice(None), kc, slice(it * P, (it + 1) * P)), part(w, slice(None), kc),
                              kc == 0, kc == T - 1)
    return last


def pe_attention(pe, L, C, x):
    B = L.banks

    def x_t(g):
        pe_transpose_rows(pe, B[0], x, C.ident).then_inc(L.x_t_psum.sem, 1)

    def qkv(g):
        pe.wait_ge(L.x_t_sb.sem, L.x_t_sb.at(g))
        pe_feature_major(pe, B[1], L.wq, L.xt).then_inc(L.qkv_psum.sem, 1)
        pe_feature_major(pe, B[2], L.wk, L.xt).then_inc(L.qkv_psum.sem, 1)
        pe_node_major(pe, B[3], L.xt, L.wv).then_inc(L.qkv_psum.sem, 1)

    def scores(g):
        pe.wait_ge(L.mask.sem, L.mask.at(g))
        pe.wait_ge(L.qk_sb.sem, L.qk_sb.at(g, 2))
        for h in range(HA):
            if h == HA - 1:
                pe.wait_ge(L.v_sb.sem, L.v_sb.at(g))
            rows = slice(DHA * (h % 2), DHA * (h % 2) + DHA)
            for it in range(T):
                out = B[h][:, it * NODES:(it + 1) * NODES]
                pe.matmul(out, C.ident_bf[:, :], L.add[:, it, :], start=True, stop=False)
                last = pe.matmul(out, L.qt[rows, h // 2, it * P:(it + 1) * P], L.kt[rows, h // 2, :],
                                 start=False, stop=True)
            last.then_inc(L.s_psum.sem, 1)

    def probs(g, heads):
        for h in heads:
            pe.wait_ge(L.p.sem, L.p.at(g, h + 1))
            for jt in range(T):
                for it in range(T):
                    last = pe.transpose(B[h][:, jt * NODES + it * P:jt * NODES + (it + 1) * P],
                                        L.e[:, h, it, jt * P:(jt + 1) * P], C.ident[:, :])
            last.then_inc(L.p_t_psum.sem, 1)

    def values(g):
        for pair in range(HA // 2):
            pe.wait_ge(L.p_t_act.sem, L.p_t_act.at(g, pair + 1))
            pe.wait_ge(L.p_t_dve.sem, L.p_t_dve.at(g, pair + 1))
            for jt in range(T):
                for half in range(2):
                    h = 2 * pair + half
                    last = pe.matmul(B[0][half * DHA:(half + 1) * DHA, pair * NODES:(pair + 1) * NODES],
                                     L.v[:, jt, h * DHA:(h + 1) * DHA], L.pt[:, h, jt, :],
                                     start=(jt == 0), stop=(jt == T - 1))
        last.then_inc(L.o_psum.sem, 1)

    def out(g):
        pe.wait_ge(L.o_sb.sem, L.o_sb.at(g))
        pe_node_major(pe, B[1], L.ot, L.wo).then_inc(L.y_psum.sem, 1)

    return x_t, qkv, scores, probs, values, out


def act_attention(act, L):
    B = L.banks

    def x_t(g):
        act.wait_ge(L.x_t_psum.sem, L.x_t_psum.at(g))
        if L.split:
            act.activation(L.xt[0], view(B[0]), ACT.Copy).then_inc(L.x_t_hi.sem, 1)
        else:
            act.activation(L.xt, view(B[0]), ACT.Copy).then_inc(L.x_t_sb.sem, 1)

    def qkv(g):
        for n, dst in enumerate((L.qt, L.kt)):
            act.wait_ge(L.qkv_psum.sem, L.qkv_psum.at(g, n + 1))
            act.activation(dst[:, :, :], view(B[1 + n]), ACT.Copy).then_inc(L.qk_sb.sem, 1)

    def scores(g):
        for h in range(HA):
            if later(g):
                act.wait_ge(L.p_t_psum.sem, L.p_t_psum.at(g - 1, h + 1))
            act.wait_ge(L.shift.sem, L.shift.at(g, h + 1))
            for it in range(T):
                last = act.activation(L.e[:, h, it, :], B[h][:, it * NODES:(it + 1) * NODES], ACT.Exp,
                                      bias=L.sh[:, h, it:it + 1], scale=DHA ** -0.5,
                                      accum_out=L.sums[:, h, it:it + 1])
            last.then_inc(L.exp.sem, 1)

    def probs(g, heads):
        for h in heads:
            if h % 2 == 0:
                if later(g):
                    act.wait_ge(L.o_psum.sem, L.o_psum.all(g - 1))
                act.wait_ge(L.p_t_psum.sem, L.p_t_psum.at(g, h + 1))
                act.activation(L.pt[:, h, :, :], view(B[h]), ACT.Copy).then_inc(L.p_t_act.sem, 1)

    def values(g):
        if L.split:
            act.wait_ge(L.o_psum.sem, L.o_psum.at(g))
            act.activation(L.ot[0], view(B[0]), ACT.Copy).then_inc(L.o_hi.sem, 1)

    return x_t, qkv, scores, probs, values


def dve_lower(dve, bank, halves):
    return dve.tensor_tensor(halves[1], view(bank), halves[0].bitcast(F32), ALU.subtract)


def dve_attention(dve, L):
    B = L.banks

    def x_t(g):
        dve.wait_ge(L.x_t_hi.sem, L.x_t_hi.at(g))
        dve_lower(dve, B[0], L.xt).then_inc(L.x_t_sb.sem, 1)

    def values(g):
        if L.split:
            dve.wait_ge(L.o_hi.sem, L.o_hi.at(g))
            dve_lower(dve, B[0], L.ot).then_inc(L.o_sb.sem, 1)
        else:
            dve.wait_ge(L.o_psum.sem, L.o_psum.at(g))
            dve.tensor_copy(L.ot, view(B[0])).then_inc(L.o_sb.sem, 1)

    def qkv(g):
        if later(g):
            dve.wait_ge(L.o_psum.sem, L.o_psum.all(g - 1))
        dve.wait_ge(L.qkv_psum.sem, L.qkv_psum.at(g, 3))
        dve.tensor_copy(L.v[:, :, :], view(B[3])).then_inc(L.v_sb.sem, 1)

    def scores(g):
        for h in range(HA):
            if later(g):
                dve.wait_ge(L.shift.sem, L.shift.at(g - 1, h + 1))
            dve.wait_ge(L.s_psum.sem, L.s_psum.at(g, h + 1))
            dve.reduce_max(L.mx[:, h, :], view(B[h]), AX_X).then_inc(L.max.sem, 1)

    def normalise(g):
        for h in range(HA):
            dve.wait_ge(L.exp.sem, L.exp.at(g, h + 1))
            dve.reciprocal(L.iv[:, h, :], L.sums[:, h, :]).then_inc(L.inv.sem, 1)
        for h in range(HA):
            dve.wait_ge(L.inv.sem, L.inv.at(g, h + 1))
            for it in range(T):
                last = dve.tensor_scalar(L.e[:, h, it, :], L.e[:, h, it, :], L.iv[:, h, it:it + 1],
                                         None, ALU.mult)
            last.then_inc(L.p.sem, 1)

    def probs(g, heads):
        for h in heads:
            if h % 2 == 1:
                if later(g):
                    dve.wait_ge(L.o_psum.sem, L.o_psum.all(g - 1))
                dve.wait_ge(L.p_t_psum.sem, L.p_t_psum.at(g, h + 1))
                dve.tensor_copy(L.pt[:, h, :, :], view(B[h])).then_inc(L.p_t_dve.sem, 1)

    def finish(g):
        dve.wait_ge(L.x_bias.sem, L.x_bias.at(g))
        dve.wait_ge(L.y_psum.sem, L.y_psum.at(g))
        dve.tensor_tensor(L.norm.r[:, :, :], view(B[1]), L.xb[:, :, :], ALU.add).then_inc(L.norm.sum.sem, 1)
        dve_norm_stats(dve, L.norm, g)

    return x_t, qkv, scores, normalise, probs, values, finish


def pool_attention(pool, L, C):
    def scores(g):
        for h in range(HA):
            if later(g):
                pool.wait_ge(L.exp.sem, L.exp.at(g - 1, h + 1))
            pool.wait_ge(L.max.sem, L.max.at(g, h + 1))
            apart(pool)
            pool.tensor_scalar(L.sh[:, h, :], L.mx[:, h, :], -(DHA ** -0.5), None, ALU.mult)\
                .then_inc(L.shift.sem, 1)

    def finish(g):
        pool_norm(pool, L.norm, C, g)

    return scores, finish


def pool_attention_mask(pool, L, g, adj):
    if later(g):
        pool.wait_ge(L.s_psum.sem, L.s_psum.all(g - 1))
    apart(pool)
    pool.tensor_scalar(L.add[:, :, :], adj[:, :, :], 1.0, -MASKED, ALU.subtract, ALU.mult)\
        .then_inc(L.mask.sem, 1)


def pool_bias(pool, L, x):
    for it in range(T):
        last = pool.tensor_tensor(L.xb[:, it, :], x[:, it, :], L.bo[:, :], ALU.add)
    last.then_inc(L.x_bias.sem, 1)


def build(nc, d, out_dram):
    with ExitStack() as ctx:
        def sb(name, shape, dt=F32):
            return ctx.enter_context(nc.sbuf_tensor(name, shape, dt))

        def signal(name, per=1):
            return Signal(ctx, nc, name, per)

        banks = [ctx.enter_context(nc.psum_tensor(f"bank{i}", [P, BANK], F32)) for i in range(8)]
        BA, BB = banks[:4], banks[4:]

        C = Names()
        C.ident, C.ident_bf = sb("ident", [P, P]), sb("ident_bf", [P, P], BF16)
        C.ones, C.minus_one, C.minus_half = sb("ones", [P, P]), sb("minus_one", [P, 16]), sb("minus_half", [P, 16])

        x_in, x_loaded = sb("x_in", [P, T, DIM]), signal("x_loaded", 16)
        adj_a, adj_a_loaded = sb("adj_a", [P, T, NODES], U8), signal("adj_a_loaded", 16)
        adj_b, adj_b_loaded = sb("adj_b", [P, T, NODES], U8), signal("adj_b_loaded", 16)
        x2, x3 = (sb(f"x{n}", [P, T, DIM])[:, :, :] for n in (2, 3))
        stored = signal("stored", 16)

        PLACE = T * NODES

        def places(name, count, dt):
            t = sb(name, [P, count * PLACE], dt)

            def at(first, n=1):
                v = t[:, first * PLACE:(first + n) * PLACE]
                if n == 1:
                    return v.rearrange("p (t n) -> p t n", t=T)
                return v.rearrange("p (h t n) -> p h t n", h=n, t=T)
            return at

        def split(at, first):
            return at(first), at(first + 1)

        def split_sb(name, shape):
            return tuple(sb(f"{name}_{half}", shape, F32R)[tuple(slice(None) for _ in shape)] for half in ("hi", "lo"))

        a32, a32r = places("a32", 10, F32), places("a32r", 22, F32R)
        b32 = places("b32", 13, F32)

        x1 = a32(9)
        A = attention_layer(ctx, nc, "l0", BA, x1, split=True)
        D = attention_layer(ctx, nc, "l3", BB, x3, split=False)
        A.e, A.pt, A.qt, A.kt, A.v, A.xb = a32(0, 4), a32(4, 4), a32(4), a32(5), a32(8), x1
        A.xt, A.ot = split(a32r, 2), split(a32r, 4)
        D.e, D.pt, D.qt, D.kt, D.v, D.xb = b32(4, 4), b32(8, 4), b32(1), b32(2), b32(3), x3
        D.xt, D.ot = b32(0), b32(4)
        A.wq, A.wk, A.wv, A.wo = (split_sb(f"l0_w{n}", [P, T, DIM]) for n in "qkvo")
        D.wq, D.wk, D.wv, D.wo = (sb(f"l3_w{n}", [P, T, DIM])[:, :, :] for n in "qkvo")

        G = Names()
        G.x_t_psum, G.x_t_hi, G.x_t_sb = signal("l1_x_t_psum"), signal("l1_x_t_hi"), signal("l1_x_t_sb")
        G.adj_psum, G.adj_sb = signal("l1_adj_psum"), signal("l1_adj_sb")
        G.adj_bf_ready = signal("l1_adj_bf")
        G.wh_psum, G.wh_f = signal("l1_wh_psum", HG), signal("l1_wh_f", HG)
        G.wh_hi, G.wh_sb = signal("l1_wh_hi", HG), signal("l1_wh_sb", HG)
        G.c_psum, G.c_sb = signal("l1_c_psum"), signal("l1_c_sb")
        G.z_psum, G.z_hi, G.z_sb = signal("l1_z_psum", HG), signal("l1_z_hi", HG), signal("l1_z_sb", HG)
        G.s_psum, G.tanh = signal("l1_s_psum", HG), signal("l1_tanh", HG)
        G.a_f, G.a_hi, G.a = signal("l1_a_f", HG), signal("l1_a_hi", HG), signal("l1_a", HG)
        G.p_psum, G.hp_hi, G.hp = signal("l1_p_psum", HG), signal("l1_hp_hi", HG), signal("l1_hp", HG)
        G.ha_psum, G.ha_sb = signal("l1_ha_psum"), signal("l1_ha_sb")
        G.ha_t_psum, G.ha_t_hi, G.ha_t_sb = signal("l1_ha_t_psum"), signal("l1_ha_t_hi"), signal("l1_ha_t_sb")
        G.hf_psum, G.gate_psum = signal("l1_hf_psum"), signal("l1_gate_psum")
        G.pre, G.gate = signal("l1_pre"), signal("l1_gate")
        G.diff, G.part, G.x_ha_done = signal("l1_diff"), signal("l1_part"), signal("l1_x_ha")
        G.norm = norm_signals(ctx, nc, "l1")
        norm_buffers(ctx, nc, G.norm, "l1", x2)
        G.adj_bf, G.adj_t = sb("g_adj_bf", [P, T, NODES], BF16), sb("g_adj_t", [P, T, NODES], BF16)
        G.c = sb("g_c", [P, T, HG])
        G.th, G.whf = a32(0, 2), a32(2, 2)
        G.pr, G.df, G.x_ha, G.ha = a32(0), a32(1), a32(2), a32(3)
        G.xt = split(a32r, 0)
        G.wh = [split(a32r, 2), split(a32r, 4)]
        G.zt = [split(a32r, 6), split(a32r, 8)]
        G.am = [split(a32r, 10), split(a32r, 12)]
        G.hpt = [split(a32r, 14 + 2 * h) for h in range(HG)]
        G.hat = split(a32r, 6)
        G.w_t = [split_sb(f"g_w_t{h}", [P, T, DIM]) for h in range(HG)]
        G.w_z = [split_sb(f"g_w_z{h}", [P, T, DIM]) for h in range(HG)]
        G.w_a = [split_sb(f"g_w_a{h}", [P, T, DIM]) for h in range(HG)]
        G.w_f, G.w_g, G.w_g2 = (split_sb(f"g_w_{n}", [P, T, DIM]) for n in ("f", "g", "g2"))
        G.b_wh, G.b_gate = sb("g_b_wh", [P, HG * DIM]), sb("g_b_gate", [P, DIM])
        G.b_z, G.b_c = sb("g_b_z", [P, T, HG]), sb("g_b_c", [P, HG])
        G.w_c = split_sb("g_w_c", [P, T, HG])

        S = Names()
        S.x_t_psum, S.x_t_sb = signal("l2_x_t_psum"), signal("l2_x_t_sb")
        S.m_psum, S.qk_psum, S.sem_psum = signal("l2_m_psum"), signal("l2_qk_psum", 2), signal("l2_sem_psum")
        S.m_sb, S.sem_sb, S.qk_sb = signal("l2_m_sb"), signal("l2_sem_sb"), signal("l2_qk_sb", 2)
        S.square, S.sumsq, S.floor, S.inorm, S.unit = (signal(f"l2_{n}") for n in ("square", "sumsq", "floor", "inorm", "unit"))
        S.unit_psum, S.unit_sb = signal("l2_unit_psum"), signal("l2_unit_sb")
        S.mask, S.keep = signal("l2_mask"), signal("l2_keep")
        S.s_psum, S.cos_psum = signal("l2_s_psum", HS), signal("l2_cos_psum", HS)
        S.max, S.shift, S.exp = signal("l2_max", HS), signal("l2_shift", HS), signal("l2_exp", HS)
        S.cut = signal("l2_cut", HS)
        S.sum_drop, S.denominator, S.factor = signal("l2_sum_drop", HS), signal("l2_denominator", HS), signal("l2_factor", HS)
        S.a = signal("l2_a", HS)
        S.a_t_psum, S.a_t_act, S.a_t_dve = signal("l2_a_t_psum", HS), signal("l2_a_t_act", HS // 2), signal("l2_a_t_dve", HS // 2)
        S.o_psum, S.o_sb = signal("l2_o_psum", 2), signal("l2_o_sb", 2)
        S.y_psum = signal("l2_y_psum")
        S.norm = norm_signals(ctx, nc, "l2")
        norm_buffers(ctx, nc, S.norm, "l2", x3)
        S.qt, S.kt, S.ut = b32(1), b32(2), b32(3)
        S.m, S.sq, S.u, S.xt, S.sem = (b32(n) for n in (4, 5, 6, 7, 0))
        S.e, S.cutp, S.at, S.ot = b32(8, 2), b32(10, 2), b32(4, 4), b32(12)
        S.ss, S.fl, S.inv = (sb(f"s_{n}", [P, T * HS]) for n in ("ss", "fl", "inv"))
        S.add, S.kp, S.drop = sb("s_add", [P, T, NODES], BF16), sb("s_kp", [P, T]), sb("s_drop", [P, T])
        S.mx, S.sh, S.sums, S.dsum, S.sd, S.den, S.fac = (
            sb(f"s_{n}", [P, HS, T]) for n in ("mx", "sh", "sums", "dsum", "sd", "den", "fac"))
        S.w_m, S.w_q, S.w_k, S.w_s = (sb(f"s_w_{n}", [P, T, DIM])[:, :, :] for n in "mqks")
        S.b_m, S.b_s = sb("s_b_m", [P, DIM]), sb("s_b_s", [P, DIM])
        S.b_q, S.b_k = sb("s_b_q", [P, T]), sb("s_b_k", [P, T])

        W = Names()
        W.w, W.attn, W.r = a32(0, 4), a32(4, 4), b32(0, 4)
        W.a_w = b32(0, 4).rearrange("p h t n -> p (h t n)").rearrange("p (t n) -> p t n", t=T)
        W.fc, W.g1, W.g2, W.map, W.q, W.k, W.gm = a32(8), a32(9), b32(4), b32(5), b32(6), b32(7), b32(8)
        W.g1_t, W.q_t, W.k_t = W.g1, W.q, W.k
        W.wq, W.wk, W.wv, W.wo = x2, x3, b32(10), b32(11)
        W.bw, W.ac, W.ab = sb("n_bw", [P, T, HG]), sb("n_ac", [P, T, HG]), sb("n_ab", [P, T, HG])
        W.mb, W.qb, W.kb, W.gb = (sb(f"n_{n}", [P, T]) for n in ("mb", "qb", "kb", "gb"))
        W.gb_rows, W.gcn, W.gcn_t = b32(9)[:, 0, :].rearrange("p (t n) -> p t n", t=T), b32(9)[:, 1, 0:P], b32(9)[:, 1, P:]
        w_loaded = ctx.enter_context(nc.semaphore("w_loaded"))
        gcn_zero = ctx.enter_context(nc.semaphore("gcn_zero"))
        const_ready = ctx.enter_context(nc.semaphore("const_ready"))
        w_psum = ctx.enter_context(nc.semaphore("w_psum"))
        w_sb = ctx.enter_context(nc.semaphore("w_sb"))
        w_hi = ctx.enter_context(nc.semaphore("w_hi"))
        w_l0 = ctx.enter_context(nc.semaphore("w_l0"))

        def rows(ap):
            return ap.rearrange("(t p) n -> p t n", p=P)

        def column(ap):
            return ap.rearrange("(t p) -> p t", p=P)

        def spread(ap):
            return ap.rearrange("(a n) -> a n", a=1).broadcast_to([P, ap.shape[0]])

        loads = [(t[:, :, :], rows(d[n])) for t, n in (
            (W.wq, "L0_gnn_Wq"), (W.wk, "L0_gnn_Wk"), (W.wv, "L0_gnn_Wv"), (W.wo, "L0_gnn_Wo"),
            (D.wq, "L3_gnn_Wq"), (D.wk, "L3_gnn_Wk"), (D.wv, "L3_gnn_Wv"), (D.wo, "L3_gnn_Wo"),
            (W.a_w, "L1_gnn_A_w"), (W.fc, "L1_gnn_fc_w"), (W.g1, "L1_gnn_g1_w"), (W.g2, "L1_gnn_g2_w"),
            (W.map, "L2_gnn_map_w"), (W.q, "L2_gnn_q_w"), (W.k, "L2_gnn_k_w"), (W.gm, "L2_gnn_gcn_map_w"))]
        for h in range(HG):
            loads.append((W.w[:, h, :, :], rows(d["L1_gnn_W"][h])))
            loads.append((W.attn[:, h, :, :], rows(d["L1_gnn_attn"][h])))
            loads.append((W.bw[:, :, h], column(d["L1_gnn_bW"][h])))
        loads += [(t[:, :], column(d[n])) for t, n in (
            (W.mb, "L2_gnn_map_b"), (W.qb, "L2_gnn_q_b"), (W.kb, "L2_gnn_k_b"), (W.gb, "L2_gnn_gcn_map_b"))]
        loads += [(t[:, :], spread(ap)) for t, ap in (
            (A.bo, d["L0_gnn_bo"]), (D.bo, d["L3_gnn_bo"]), (S.b_m, d["L2_gnn_map_b"]), (G.b_gate, d["L1_gnn_gbias"]),
            (G.b_wh, d["L1_gnn_bW"].rearrange("h o -> (h o)")))]
        n_loads = len(loads) + P // DHS

        block = ctx.enter_context(nc.Block())

        def pe_setup(pe):
            done = [0]

            def step(products, needs=0):
                n = done[0]
                if n >= 8:
                    needs = max(needs, n - 7)
                if needs:
                    pe.wait_ge(w_sb, needs)
                products(banks[n % 8]).then_inc(w_psum, 1)
                done[0] += 1
                return n + 1

            def mm_pairs(b, lhs, rhs_of, n=DIM):
                for mt in range(T):
                    for kc in range(T):
                        last = pe.matmul(b[:, mt * n:(mt + 1) * n], lhs[:, kc, mt * P:(mt + 1) * P], rhs_of(kc),
                                         start=(kc == 0), stop=(kc == T - 1))
                return last

            pe.wait_ge(w_loaded, 16 * n_loads)
            pe.wait_ge(const_ready, 5)
            for h in range(HG):
                step(lambda b: pe_transpose_rows(pe, b, W.w[:, h, :, :], C.ident))
            for cc in range(HG):
                step(lambda b: pe_transpose_rows(pe, b, W.a_w[:, :, cc * DIM:(cc + 1) * DIM], C.ident))
            for h in range(HG):
                r_done = step(lambda b: mm_pairs(b, W.attn[:, h, :, :], lambda kc: W.w[:, h, kc, :]))
            for h in range(HG):
                step(lambda b: mm_pairs(b, W.w[:, h, :, :], lambda kc: W.r[:, h, kc, :]), needs=r_done)
            for src in (W.fc, W.g2, W.g1, W.map, W.q, W.k):
                t_done = step(lambda b: pe_transpose_rows(pe, b, src, C.ident))
            step(lambda b: mm_pairs(b, W.fc, lambda kc: W.g1_t[:, kc, :]), needs=t_done)
            step(lambda b: mm_pairs(b, W.map, lambda kc: W.q_t[:, kc, :]))
            step(lambda b: mm_pairs(b, W.map, lambda kc: W.k_t[:, kc, :]))
            gcn_done = step(lambda b: pe.transpose(b[:, 0:P], W.gcn, C.ident[:, :]))

            def sem_weight(b):
                for kc in range(T):
                    for jt in range(T):
                        last = pe.matmul(b[:, kc * DIM + jt * P:kc * DIM + (jt + 1) * P],
                                         W.gm[:, jt, kc * P:(kc + 1) * P], W.gcn_t, start=True, stop=True)
                return last

            def sem_bias(b):
                for jt in range(T):
                    last = pe.matmul(b[:, jt * P:(jt + 1) * P], W.gb_rows[:, jt, :], W.gcn_t, start=True, stop=True)
                return last

            def columns(b, lhs_of, rhs_of, heads):
                for t in range(T):
                    for h in range(heads):
                        for kc in range(T):
                            last = pe.matmul(b[:, t * heads + h:t * heads + h + 1], lhs_of(h, kc, t), rhs_of(h, kc),
                                             start=(kc == 0), stop=(kc == T - 1))
                return last

            step(sem_weight, needs=gcn_done)
            step(sem_bias)
            step(lambda b: columns(b, lambda h, kc, t: W.q_t[:, kc, t * P:(t + 1) * P], lambda h, kc: W.mb[:, kc:kc + 1], 1))
            step(lambda b: columns(b, lambda h, kc, t: W.k_t[:, kc, t * P:(t + 1) * P], lambda h, kc: W.mb[:, kc:kc + 1], 1))
            step(lambda b: columns(b, lambda h, kc, t: W.r[:, h, kc, t * P:(t + 1) * P], lambda h, kc: W.bw[:, kc, h:h + 1], HG))
            a_done = step(lambda b: columns(b, lambda h, kc, t: W.attn[:, h, kc, t * P:(t + 1) * P],
                                            lambda h, kc: W.bw[:, kc, h:h + 1], HG))
            step(lambda b: columns(b, lambda h, kc, t: W.w[:, h, kc, t * P:(t + 1) * P],
                                   lambda h, kc: W.ac[:, kc, h:h + 1], HG), needs=a_done)

            def c_bias(b):
                for kc in range(T):
                    last = pe.matmul(b[:, 0:HG], C.ones[:, :], W.ab[:, kc, :], start=(kc == 0), stop=(kc == T - 1))
                return last

            step(c_bias, needs=a_done + 1)

        def dve_setup(dve):
            done, halves = [0], [0]

            def copy(dst, width=2 * DIM, inner=DIM, plus=None):
                n = done[0]
                dve.wait_ge(w_psum, n + 1)
                src = banks[n % 8][:, 0:width]
                if inner:
                    src = src.rearrange("p (a n) -> p a n", n=inner)
                if isinstance(dst, tuple):
                    halve(dst, src)
                elif plus is None:
                    dve.tensor_copy(dst, src).then_inc(w_sb, 1)
                else:
                    dve.tensor_tensor(dst, src, plus, ALU.add).then_inc(w_sb, 1)
                done[0] += 1

            def halve(dst, src, ready=w_sb):
                halves[0] += 1
                dve.tensor_copy(dst[0], src).then_inc(w_hi, 1)
                dve.wait_ge(w_hi, halves[0])
                dve.tensor_tensor(dst[1], src, dst[0].bitcast(F32), ALU.subtract).then_inc(ready, 1)

            dve.wait_ge(w_loaded, 16 * n_loads)
            for jt in range(T):
                dve.tensor_scalar(W.gb_rows[:, jt, :], C.ones[:, :], W.gb[:, jt:jt + 1], None, ALU.mult)
            for h in range(HG):
                copy(G.w_t[h])
            for h in range(HG):
                copy(G.w_a[h])
            for h in range(HG):
                copy(W.r[:, h, :, :])
            for h in range(HG):
                copy(G.w_z[h])
            for dst in (G.w_f, G.w_g2, W.g1_t, S.w_m, W.q_t, W.k_t):
                copy(dst)
            for dst in (G.w_g, S.w_q, S.w_k):
                copy(dst)
            copy(W.gcn_t, P, None)
            copy(S.w_s)
            copy(S.b_s[:, :], DIM, None)
            copy(S.b_q[:, :], T, None, W.qb[:, :])
            copy(S.b_k[:, :], T, None, W.kb[:, :])
            for dst, src in ((A.wq, W.wq), (A.wk, W.wk), (A.wv, W.wv), (A.wo, W.wo)):
                halve(dst, src, w_l0)
            copy(G.b_z[:, :, :], T * HG, HG)
            copy(W.ac[:, :, :], T * HG, HG)
            dve.wait_ge(w_sb, done[0])
            dve.tensor_tensor(W.ab[:, :, :], W.ac[:, :, :], W.bw[:, :, :], ALU.mult).then_inc(w_sb, 1)
            dve.wait_ge(w_psum, done[0] + 1)
            halve(G.w_c, banks[done[0] % 8][:, 0:T * HG].rearrange("p (a n) -> p a n", n=HG))
            dve.wait_ge(w_psum, done[0] + 2)
            dve.tensor_copy(G.b_c[:, :], banks[(done[0] + 1) % 8][:, 0:HG]).then_inc(w_sb, 1)
            done[0] += 3
            return done[0]

        SETUP_COPIES = 4 * HG + 6 + 3 + 3 + 2 + 2 + 3

        def loop(eng, slot_a, slot_b):
            def body(t):
                for stage, behind in SCHEDULE:
                    g = t - behind if behind else t
                    if isinstance(g, int) and not 0 <= g < GRAPHS:
                        continue
                    (slot_a if stage[0] in "ag" else slot_b)(stage, g)

            for t in range(LAG + 1):
                body(t)
            with eng.Fori(LAG + 1, GRAPHS) as t:
                body(t)
            for t in range(GRAPHS, GRAPHS + LAG):
                body(t)

        @block.sync
        def _(sp):
            sp.wait_ge(gcn_zero, 1)
            for n in range(P // DHS):
                sp.dma_start(W.gcn[n * DHS:(n + 1) * DHS, n * DHS:(n + 1) * DHS], d["L2_gnn_gcn_W"]).then_inc(w_loaded, 16)
            for dst, src in loads:
                sp.dma_start(dst, src, allow_slow_non_contiguous=True).then_inc(w_loaded, 16)

            def load_a(g):
                if later(g):
                    sp.wait_ge(A.x_bias.sem, A.x_bias.all(g - 1))
                if later(g):
                    sp.wait_ge(A.x_t_psum.sem, A.x_t_psum.all(g - 1))
                apart(sp)
                sp.dma_start(x_in[:, :, :], d["x"][g].rearrange("(t p) n -> p t n", p=P)).then_inc(x_loaded.sem, 16)
                if later(g):
                    sp.wait_ge(G.adj_bf_ready.sem, G.adj_bf_ready.all(g - 1))
                apart(sp)
                sp.dma_start(adj_a[:, :, :], d["adj"][g].rearrange("(t p) n -> p t n", p=P)).then_inc(adj_a_loaded.sem, 16)

            def load_b(g):
                if later(g):
                    sp.wait_ge(D.mask.sem, D.mask.all(g - 1))
                apart(sp)
                sp.dma_start(adj_b[:, :, :], d["adj"][g].rearrange("(t p) n -> p t n", p=P)).then_inc(adj_b_loaded.sem, 16)

            def store(g):
                sp.wait_ge(D.norm.out.sem, D.norm.out.at(g))
                apart(sp)
                sp.dma_start(out_dram[g].rearrange("(t p) n -> p t n", p=P), x3).then_inc(stored.sem, 16)

            load_a(0)
            load_b(0)
            load_a(1)
            load_a(2)
            load_b(1)
            with sp.Fori(2, GRAPHS - 1) as t:
                store(t - 2)
                load_a(t + 1)
                load_b(t)
            store(GRAPHS - 3)
            load_b(GRAPHS - 1)
            store(GRAPHS - 2)
            store(GRAPHS - 1)
            sp.wait_ge(stored.sem, 16 * GRAPHS)

        @block.tensor
        def _(pe):
            pe_setup(pe)
            pe.wait_ge(w_sb, SETUP_COPIES)
            pe.wait_ge(w_l0, 4)

            a_x_t, a_qkv, a_scores, a_probs, a_values, a_out = pe_attention(pe, A, C, x_in)
            d_x_t, d_qkv, d_scores, d_probs, d_values, d_out = pe_attention(pe, D, C, x3)

            def g_x_t(g):
                pe.wait_ge(G.adj_bf_ready.sem, G.adj_bf_ready.at(g))
                adj_bank = BA[3][:, 0:NODES].bitcast(BF16)
                for mt in range(T):
                    for nt in range(T):
                        last = pe.transpose(adj_bank[:, mt * NODES + nt * P:mt * NODES + (nt + 1) * P],
                                            G.adj_bf[:, nt, mt * P:(mt + 1) * P], C.ident_bf[:, :])
                last.then_inc(G.adj_psum.sem, 1)
                pe.wait_ge(A.norm.out.sem, A.norm.out.at(g))
                pe_transpose_rows(pe, BA[0], x1, C.ident).then_inc(G.x_t_psum.sem, 1)

            def g_wh(g, h):
                if h == 0:
                    pe.wait_ge(G.x_t_sb.sem, G.x_t_sb.at(g))
                else:
                    pe.wait_ge(G.wh_f.sem, G.wh_f.at(g, h))
                pe_node_major(pe, BA[1], G.xt, G.w_t[h]).then_inc(G.wh_psum.sem, 1)

            def g_c(g):
                for it in range(T):
                    for kc in range(T):
                        last = pe_product(pe, BA[2][:, it * HG:(it + 1) * HG],
                                          part(G.xt, slice(None), kc, slice(it * P, (it + 1) * P)),
                                          part(G.w_c, slice(None), kc), kc == 0, kc == T - 1)
                last.then_inc(G.c_psum.sem, 1)

            def g_z(g, h):
                if h:
                    pe.wait_ge(G.z_sb.sem, G.z_sb.at(g, h))
                pe_feature_major(pe, BA[0], G.w_z[h], G.xt).then_inc(G.z_psum.sem, 1)

            def g_s(g, h):
                pe.wait_ge(G.z_sb.sem, G.z_sb.at(g, h + 1))
                if h == 0:
                    pe.wait_ge(G.c_sb.sem, G.c_sb.at(g))
                else:
                    pe.wait_ge(G.tanh.sem, G.tanh.at(g, h))
                pe_node_major(pe, BA[2], G.zt[h % 2], G.xt).then_inc(G.s_psum.sem, 1)

            def g_p(g, h):
                pe.wait_ge(G.a.sem, G.a.at(g, h + 1))
                pe.wait_ge(G.wh_sb.sem, G.wh_sb.at(g, h + 1))
                if h == 0:
                    pe.wait_ge(G.adj_sb.sem, G.adj_sb.at(g))
                else:
                    pe.wait_ge(G.hp.sem, G.hp.at(g, h))
                pe_feature_major(pe, BA[3], G.wh[h % 2], G.am[h % 2]).then_inc(G.p_psum.sem, 1)

            def g_ha(g, nt, heads):
                for h in heads:
                    for kc in range(T):
                        last = pe_product(pe, BA[1 + nt][:, 0:DIM],
                                          part(G.hpt[h], slice(None), kc, slice(nt * P, (nt + 1) * P)),
                                          part(G.w_a[h], slice(None), kc), h == 0 and kc == 0,
                                          h == HG - 1 and kc == T - 1)
                return last

            def g_ha_t(g):
                pe.wait_ge(G.ha_sb.sem, G.ha_sb.at(g))
                pe_transpose_rows(pe, BA[3], G.ha, C.ident).then_inc(G.ha_t_psum.sem, 1)

            def g_gate(g):
                pe.wait_ge(G.ha_t_sb.sem, G.ha_t_sb.at(g))
                for nt in range(T):
                    for kc in range(2 * T):
                        src, w = ((G.xt, G.w_g), (G.hat, G.w_g2))[kc // T]
                        last = pe_product(pe, BA[1][:, nt * DIM:(nt + 1) * DIM],
                                          part(src, slice(None), kc % T, slice(nt * P, (nt + 1) * P)),
                                          part(w, slice(None), kc % T), kc == 0, kc == 2 * T - 1)
                last.then_inc(G.gate_psum.sem, 1)

            def slot_a(stage, g):
                if stage == "a_x_t":
                    pe.wait_ge(x_loaded.sem, x_loaded.all(g))
                    if later(g):
                        pe.wait_ge(G.diff.sem, G.diff.all(g - 1))
                    a_x_t(g)
                elif stage == "a_qkv":
                    if later(g):
                        pe.wait_ge(G.pre.sem, G.pre.all(g - 1))
                    a_qkv(g)
                elif stage == "a_scores":
                    if later(g):
                        pe.wait_ge(G.norm.sum.sem, G.norm.sum.all(g - 1))
                    a_scores(g)
                elif stage == "a_probs_01":
                    a_probs(g, (0, 1))
                elif stage == "a_probs_23":
                    a_probs(g, (2, 3))
                elif stage == "a_values":
                    a_values(g)
                elif stage == "a_out":
                    a_out(g)
                elif stage == "g_x_t":
                    g_x_t(g)
                elif stage == "g_0":
                    g_wh(g, 0)
                    g_z(g, 0)
                    g_c(g)
                elif stage == "g_1":
                    g_s(g, 0)
                    g_wh(g, 1)
                    g_z(g, 1)
                elif stage.startswith("g_p"):
                    g_p(g, int(stage[4:]))
                elif stage == "g_2":
                    g_s(g, 1)
                    g_wh(g, 2)
                    g_z(g, 2)
                elif stage == "g_3":
                    g_s(g, 2)
                    g_wh(g, 3)
                    g_z(g, 3)
                elif stage == "g_4":
                    g_s(g, 3)
                    pe_node_major(pe, BA[0], G.xt, G.w_f).then_inc(G.hf_psum.sem, 1)
                elif stage == "g_ha_0":
                    pe.wait_ge(G.hp.sem, G.hp.at(g, HG - 1))
                    pe.wait_ge(G.wh_f.sem, G.wh_f.at(g, HG))
                    g_ha(g, 0, range(HG - 1))
                elif stage == "g_ha_1":
                    pe.wait_ge(G.tanh.sem, G.tanh.at(g, HG))
                    g_ha(g, 1, range(HG - 1))
                    pe.wait_ge(G.hp.sem, G.hp.at(g, HG))
                    g_ha(g, 0, (HG - 1,))
                    g_ha(g, 1, (HG - 1,)).then_inc(G.ha_psum.sem, 1)
                elif stage == "g_ha_t":
                    g_ha_t(g)
                elif stage == "g_gate":
                    g_gate(g)

            def b_x_t(g):
                pe.wait_ge(G.norm.out.sem, G.norm.out.at(g))
                pe_transpose_rows(pe, BB[2], x2, C.ident).then_inc(S.x_t_psum.sem, 1)

            def b_project(g):
                pe.wait_ge(S.x_t_sb.sem, S.x_t_sb.at(g))
                if later(g):
                    pe.wait_ge(D.norm.sum.sem, D.norm.sum.all(g - 1))
                pe_node_major(pe, BB[1], S.xt, S.w_m).then_inc(S.m_psum.sem, 1)
                pe_feature_major(pe, BB[2], S.w_q, S.xt).then_inc(S.qk_psum.sem, 1)
                pe_feature_major(pe, BB[3], S.w_k, S.xt).then_inc(S.qk_psum.sem, 1)
                pe_node_major(pe, BB[0], S.xt, S.w_s).then_inc(S.sem_psum.sem, 1)

            def b_unit_t(g):
                pe.wait_ge(S.unit.sem, S.unit.at(g))
                pe_transpose_rows(pe, BB[1], S.u, C.ident).then_inc(S.unit_psum.sem, 1)

            def b_scores(g, h):
                if h == 0:
                    pe.wait_ge(S.mask.sem, S.mask.at(g))
                    pe.wait_ge(S.qk_sb.sem, S.qk_sb.at(g, 2))
                    pe.wait_ge(S.sem_sb.sem, S.sem_sb.at(g))
                elif h == 1:
                    pe.wait_ge(S.unit_sb.sem, S.unit_sb.at(g))
                else:
                    pe.wait_ge(S.exp.sem, S.exp.at(g, h - 1))
                rows = slice(DHS * (h % 4), DHS * (h % 4) + DHS)
                for it in range(T):
                    out = BB[h % 2][:, it * NODES:(it + 1) * NODES]
                    pe.matmul(out, C.ident_bf[:, :], S.add[:, it, :], start=True, stop=False)
                    last = pe.matmul(out, S.qt[rows, h // 4, it * P:(it + 1) * P], S.kt[rows, h // 4, :],
                                     start=False, stop=True)
                last.then_inc(S.s_psum.sem, 1)

            def b_cos(g, h):
                if h == 0:
                    pe.wait_ge(S.unit_sb.sem, S.unit_sb.at(g))
                    pe.wait_ge(S.qk_sb.sem, S.qk_sb.at(g, 2))
                else:
                    pe.wait_ge(S.cut.sem, S.cut.at(g, h))
                rows = slice(DHS * (h % 4), DHS * (h % 4) + DHS)
                for it in range(T):
                    last = pe.matmul(BB[2][:, it * NODES:(it + 1) * NODES], S.ut[rows, h // 4, it * P:(it + 1) * P],
                                     S.ut[rows, h // 4, :], start=True, stop=True)
                last.then_inc(S.cos_psum.sem, 1)

            def b_transpose(g, h):
                pe.wait_ge(S.a.sem, S.a.at(g, h + 1))
                if h == 4:
                    pe.wait_ge(S.o_sb.sem, S.o_sb.at(g, 1))
                elif h % 2:
                    pe.wait_ge(S.a_t_act.sem, S.a_t_act.at(g, (h + 1) // 2))
                elif h:
                    pe.wait_ge(S.a_t_dve.sem, S.a_t_dve.at(g, h // 2))
                for jt in range(T):
                    for it in range(T):
                        last = pe.transpose(BB[3][:, jt * NODES + it * P:jt * NODES + (it + 1) * P],
                                            S.cutp[:, h % 2, it, jt * P:(jt + 1) * P], C.ident[:, :])
                last.then_inc(S.a_t_psum.sem, 1)

            def b_values(g, half):
                pe.wait_ge(S.a_t_act.sem, S.a_t_act.at(g, 2 * half + 2))
                pe.wait_ge(S.a_t_dve.sem, S.a_t_dve.at(g, 2 * half + 2))
                for jt in range(T):
                    for n in range(4):
                        h = 4 * half + n
                        last = pe.matmul(BB[3][n * DHS:(n + 1) * DHS, 0:NODES], S.sem[:, jt, h * DHS:(h + 1) * DHS],
                                         S.at[:, n, jt, :], start=(jt == 0), stop=(jt == T - 1))
                last.then_inc(S.o_psum.sem, 1)

            def b_out(g):
                pe.wait_ge(S.o_sb.sem, S.o_sb.at(g, 2))
                pe_transpose_rows(pe, BB[0], S.ot, C.ident).then_inc(S.y_psum.sem, 1)

            def b_head(g, n):
                if n == 0:
                    b_scores(g, 0)
                    b_scores(g, 1)
                    b_cos(g, 0)
                else:
                    if n in (5, 9):
                        b_values(g, n // 8)
                    if n + 1 < HS:
                        b_scores(g, n + 1)
                    if n < HS:
                        b_cos(g, n)
                    if 0 <= n - 1 < HS:
                        b_transpose(g, n - 1)

            def slot_b(stage, g):
                if stage == "b_x_t":
                    b_x_t(g)
                elif stage == "b_project":
                    b_project(g)
                elif stage == "b_unit_t":
                    b_unit_t(g)
                elif stage.startswith("b_head"):
                    b_head(g, int(stage[7:]))
                elif stage == "b_out":
                    b_out(g)
                elif stage == "d_x_t":
                    pe.wait_ge(S.norm.out.sem, S.norm.out.at(g))
                    d_x_t(g)
                elif stage == "d_qkv":
                    d_qkv(g)
                elif stage == "d_scores":
                    d_scores(g)
                elif stage == "d_probs_01":
                    d_probs(g, (0, 1))
                elif stage == "d_probs_23":
                    d_probs(g, (2, 3))
                elif stage == "d_values":
                    d_values(g)
                elif stage == "d_out":
                    d_out(g)

            loop(pe, slot_a, slot_b)

        @block.scalar
        def _(act):
            act.wait_ge(w_sb, SETUP_COPIES)
            a_x_t, a_qkv, a_scores, a_probs, a_values = act_attention(act, A)
            d_x_t, d_qkv, d_scores, d_probs, _ = act_attention(act, D)

            def g_z(g, h):
                act.wait_ge(G.z_psum.sem, G.z_psum.at(g, h + 1))
                for dt in range(T):
                    last = act.activation(G.zt[h % 2][0][:, dt, :], BA[0][:, dt * NODES:(dt + 1) * NODES], ACT.Identity,
                                          bias=G.b_z[:, dt, h:h + 1])
                last.then_inc(G.z_hi.sem, 1)

            def g_s(g, h):
                act.wait_ge(G.s_psum.sem, G.s_psum.at(g, h + 1))
                if h == 0:
                    act.wait_ge(G.c_sb.sem, G.c_sb.at(g))
                if h >= 2:
                    act.wait_ge(G.a.sem, G.a.at(g, h - 1))
                elif later(g):
                    act.wait_ge(G.a.sem, G.a.all(g - 1))
                for mt in range(T):
                    last = act.activation(G.th[:, h % 2, mt, :], BA[2][:, mt * NODES:(mt + 1) * NODES], ACT.Tanh,
                                          bias=G.c[:, mt, h:h + 1])
                last.then_inc(G.tanh.sem, 1)

            def g_a(g, h):
                act.wait_ge(G.a_f.sem, G.a_f.at(g, h + 1))
                act.activation(G.am[h % 2][0], G.th[:, h % 2, :, :], ACT.Copy).then_inc(G.a_hi.sem, 1)

            def g_wh(g, h):
                act.wait_ge(G.wh_f.sem, G.wh_f.at(g, h + 1))
                act.activation(G.wh[h % 2][0], G.whf[:, h % 2, :, :], ACT.Copy).then_inc(G.wh_hi.sem, 1)

            def g_hp(g, h):
                act.wait_ge(G.p_psum.sem, G.p_psum.at(g, h + 1))
                act.activation(G.hpt[h][0], view(BA[3]), ACT.Relu).then_inc(G.hp_hi.sem, 1)

            def slot_a(stage, g):
                if stage == "a_x_t":
                    a_x_t(g)
                elif stage == "a_qkv":
                    a_qkv(g)
                elif stage == "a_exps":
                    a_scores(g)
                elif stage == "a_probs_01":
                    a_probs(g, (0, 1))
                elif stage == "a_probs_23":
                    a_probs(g, (2, 3))
                elif stage == "a_values":
                    a_values(g)
                elif stage == "g_x_t":
                    act.wait_ge(G.x_t_psum.sem, G.x_t_psum.at(g))
                    act.activation(G.xt[0], view(BA[0]), ACT.Copy).then_inc(G.x_t_hi.sem, 1)
                elif stage == "g_0":
                    g_wh(g, 0)
                    g_z(g, 0)
                elif stage == "g_1":
                    g_s(g, 0)
                    g_a(g, 0)
                    g_wh(g, 1)
                    g_z(g, 1)
                elif stage.startswith("g_p"):
                    g_hp(g, int(stage[4:]))
                elif stage == "g_2":
                    g_s(g, 1)
                    g_a(g, 1)
                    g_wh(g, 2)
                    g_z(g, 2)
                elif stage == "g_3":
                    g_s(g, 2)
                    g_a(g, 2)
                    g_wh(g, 3)
                    g_z(g, 3)
                elif stage == "g_4":
                    g_s(g, 3)
                    g_a(g, 3)
                elif stage == "g_ha_1":
                    act.wait_ge(G.ha_psum.sem, G.ha_psum.at(g))
                    if later(g):
                        act.wait_ge(G.diff.sem, G.diff.all(g - 1))
                    if later(g):
                        act.wait_ge(G.x_ha_done.sem, G.x_ha_done.all(g - 1))
                    for nt in range(T):
                        last = act.activation(G.ha[:, nt, :], BA[1 + nt][:, 0:DIM], ACT.Copy)
                    last.then_inc(G.ha_sb.sem, 1)
                elif stage == "g_ha_t":
                    act.wait_ge(G.ha_t_psum.sem, G.ha_t_psum.at(g))
                    act.activation(G.hat[0], view(BA[3]), ACT.Copy).then_inc(G.ha_t_hi.sem, 1)
                elif stage == "g_gate":
                    act.wait_ge(G.pre.sem, G.pre.at(g))
                    act.activation(G.pr, G.pr, ACT.Tanh, scale=0.5).then_inc(G.gate.sem, 1)

            def exps(g, h):
                act.wait_ge(S.shift.sem, S.shift.at(g, h + 1))
                if h >= 2:
                    act.wait_ge(S.cut.sem, S.cut.at(g, h - 1))
                else:
                    if later(g):
                        act.wait_ge(S.cut.sem, S.cut.all(g - 1))
                for it in range(T):
                    last = act.activation(S.e[:, h % 2, it, :], BB[h % 2][:, it * NODES:(it + 1) * NODES], ACT.Exp,
                                          bias=S.sh[:, h, it:it + 1], scale=DHS ** -0.5, accum_out=S.sums[:, h, it:it + 1])
                last.then_inc(S.exp.sem, 1)

            def copy_t(g, h):
                if h % 2 == 0:
                    act.wait_ge(S.a_t_psum.sem, S.a_t_psum.at(g, h + 1))
                    act.activation(S.at[:, h % 4, :, :], view(BB[3]), ACT.Copy).then_inc(S.a_t_act.sem, 1)

            def relu(g, half):
                act.wait_ge(S.o_psum.sem, S.o_psum.at(g, half + 1))
                act.activation(S.ot[:, half, :], BB[3][:, 0:NODES], ACT.Relu).then_inc(S.o_sb.sem, 1)

            def slot_b(stage, g):
                if stage == "b_x_t":
                    act.wait_ge(S.x_t_psum.sem, S.x_t_psum.at(g))
                    act.activation(S.xt, view(BB[2]), ACT.Copy).then_inc(S.x_t_sb.sem, 1)
                elif stage == "b_project":
                    for n, (dst, bias) in enumerate(((S.qt, S.b_q), (S.kt, S.b_k))):
                        act.wait_ge(S.qk_psum.sem, S.qk_psum.at(g, n + 1))
                        for jt in range(T):
                            last = act.activation(dst[:, jt, :], BB[2 + n][:, jt * NODES:(jt + 1) * NODES], ACT.Identity,
                                                  bias=bias[:, jt:jt + 1])
                        last.then_inc(S.qk_sb.sem, 1)
                elif stage == "b_unit_t":
                    act.wait_ge(S.unit_psum.sem, S.unit_psum.at(g))
                    act.activation(S.ut[:, :, :], view(BB[1]), ACT.Copy).then_inc(S.unit_sb.sem, 1)
                elif stage.startswith("b_head"):
                    n = int(stage[7:])
                    if n in (5, 9):
                        relu(g, n // 8)
                    if n == 0:
                        exps(g, 0)
                    if n + 1 < HS:
                        exps(g, n + 1)
                    if 1 <= n <= HS:
                        copy_t(g, n - 1)
                elif stage == "d_x_t":
                    d_x_t(g)
                elif stage == "d_qkv":
                    d_qkv(g)
                elif stage == "d_scores":
                    d_scores(g)
                elif stage == "d_probs_01":
                    d_probs(g, (0, 1))
                elif stage == "d_probs_23":
                    d_probs(g, (2, 3))

            loop(act, slot_a, slot_b)

        @block.vector
        def _(dve):
            dve.wait_ge(const_ready, 5)
            copies = dve_setup(dve)
            assert copies == SETUP_COPIES, copies
            dve.wait_ge(w_sb, SETUP_COPIES)
            dve.wait_ge(w_l0, 4)
            a_x_t, a_qkv, a_scores, a_normalise, a_probs, a_values, a_finish = dve_attention(dve, A)
            _, d_qkv, d_scores, d_normalise, d_probs, d_values, d_finish = dve_attention(dve, D)

            def g_wh(g, h):
                dve.wait_ge(G.wh_psum.sem, G.wh_psum.at(g, h + 1))
                if h >= 2:
                    dve.wait_ge(G.wh_sb.sem, G.wh_sb.at(g, h - 1))
                for it in range(T):
                    last = dve.tensor_tensor(G.whf[:, h % 2, it, :], BA[1][:, it * DIM:(it + 1) * DIM],
                                             G.b_wh[:, h * DIM:(h + 1) * DIM], ALU.add)
                last.then_inc(G.wh_f.sem, 1)

            def g_z(g, h):
                dve.wait_ge(G.z_hi.sem, G.z_hi.at(g, h + 1))
                for dt in range(T):
                    last = dve.scalar_tensor_tensor(G.zt[h % 2][1][:, dt, :], BA[0][:, dt * NODES:(dt + 1) * NODES],
                                                    G.b_z[:, dt, h:h + 1], G.zt[h % 2][0][:, dt, :].bitcast(F32),
                                                    ALU.add, ALU.subtract)
                last.then_inc(G.z_sb.sem, 1)

            def g_a(g, h):
                dve.wait_ge(G.tanh.sem, G.tanh.at(g, h + 1))
                if h == 0:
                    dve.wait_ge(G.adj_sb.sem, G.adj_sb.at(g))
                dve.tensor_tensor(G.th[:, h % 2, :, :], G.th[:, h % 2, :, :], G.adj_t[:, :, :], ALU.mult)\
                    .then_inc(G.a_f.sem, 1)

            def g_hp(g, h):
                dve.wait_ge(G.hp_hi.sem, G.hp_hi.at(g, h + 1))
                dve.scalar_tensor_tensor(G.hpt[h][1], view(BA[3]), 0.0, G.hpt[h][0].bitcast(F32),
                                         ALU.max, ALU.subtract).then_inc(G.hp.sem, 1)

            def slot_a(stage, g):
                if stage == "a_x_t":
                    a_x_t(g)
                elif stage == "a_qkv":
                    a_qkv(g)
                elif stage == "a_values":
                    a_values(g)
                elif stage == "a_scores":
                    a_scores(g)
                elif stage == "a_norm":
                    a_normalise(g)
                elif stage == "a_probs_01":
                    a_probs(g, (0, 1))
                elif stage == "a_probs_23":
                    a_probs(g, (2, 3))
                elif stage == "a_sum":
                    a_finish(g)
                elif stage == "a_norm_out":
                    dve_norm_out(dve, A.norm, g)
                elif stage == "g_x_t":
                    dve.wait_ge(G.adj_psum.sem, G.adj_psum.at(g))
                    dve.tensor_copy(G.adj_t[:, :, :], BA[3][:, 0:NODES].bitcast(BF16).rearrange("p (a n) -> p a n", n=NODES))\
                        .then_inc(G.adj_sb.sem, 1)
                    dve.wait_ge(G.x_t_hi.sem, G.x_t_hi.at(g))
                    dve_lower(dve, BA[0], G.xt).then_inc(G.x_t_sb.sem, 1)
                elif stage == "g_0":
                    g_wh(g, 0)
                    g_z(g, 0)
                    dve.wait_ge(G.c_psum.sem, G.c_psum.at(g))
                    if later(g):
                        dve.wait_ge(G.tanh.sem, G.tanh.all(g - 1))
                    for it in range(T):
                        last = dve.tensor_tensor(G.c[:, it, :], BA[2][:, it * HG:(it + 1) * HG], G.b_c[:, :], ALU.add)
                    last.then_inc(G.c_sb.sem, 1)
                elif stage == "g_1":
                    g_a(g, 0)
                    g_wh(g, 1)
                    g_z(g, 1)
                elif stage.startswith("g_p"):
                    g_hp(g, int(stage[4:]))
                elif stage == "g_2":
                    g_a(g, 1)
                    g_wh(g, 2)
                    g_z(g, 2)
                elif stage == "g_3":
                    g_a(g, 2)
                    g_wh(g, 3)
                    g_z(g, 3)
                elif stage == "g_4":
                    g_a(g, 3)
                elif stage == "g_ha_t":
                    dve.wait_ge(G.ha_sb.sem, G.ha_sb.at(g))
                    dve.wait_ge(G.hf_psum.sem, G.hf_psum.at(g))
                    dve.tensor_tensor(G.df, view(BA[0]), G.ha, ALU.subtract).then_inc(G.diff.sem, 1)
                    dve.wait_ge(G.ha_t_hi.sem, G.ha_t_hi.at(g))
                    dve_lower(dve, BA[3], G.hat).then_inc(G.ha_t_sb.sem, 1)
                elif stage == "g_gate":
                    dve.wait_ge(G.gate_psum.sem, G.gate_psum.at(g))
                    for nt in range(T):
                        last = dve.tensor_tensor(G.pr[:, nt, :], BA[1][:, nt * DIM:(nt + 1) * DIM], G.b_gate[:, :], ALU.add)
                    last.then_inc(G.pre.sem, 1)
                elif stage == "g_mix":
                    dve.wait_ge(G.x_ha_done.sem, G.x_ha_done.at(g))
                    dve.wait_ge(G.diff.sem, G.diff.at(g))
                    dve.wait_ge(G.gate.sem, G.gate.at(g))
                    dve.scalar_tensor_tensor(G.df, G.pr, 1.0, G.df, ALU.add, ALU.mult).then_inc(G.part.sem, 1)
                    dve.wait_ge(G.part.sem, G.part.at(g))
                    if later(g):
                        dve.wait_ge(S.x_t_psum.sem, S.x_t_psum.all(g - 1))
                        dve.wait_ge(S.norm.sum.sem, S.norm.sum.all(g - 1))
                    dve.scalar_tensor_tensor(G.norm.r, G.df, 0.5, G.x_ha, ALU.mult, ALU.add)\
                        .then_inc(G.norm.sum.sem, 1)
                    dve_norm_stats(dve, G.norm, g)
                elif stage == "g_norm_out":
                    dve_norm_out(dve, G.norm, g)

            def cut(g, h):
                dve.wait_ge(S.cos_psum.sem, S.cos_psum.at(g, h + 1))
                dve.wait_ge(S.exp.sem, S.exp.at(g, h + 1))
                if h >= 2:
                    dve.wait_ge(S.a_t_psum.sem, S.a_t_psum.at(g, h - 1))
                else:
                    if later(g):
                        dve.wait_ge(S.a_t_psum.sem, S.a_t_psum.all(g - 1))
                for it in range(T):
                    last = dve.scalar_tensor_tensor(S.cutp[:, h % 2, it, :], BB[2][:, it * NODES:(it + 1) * NODES], COS_MIN,
                                                    S.e[:, h % 2, it, :], ALU.is_gt, ALU.mult, accum_out=S.dsum[:, h, it:it + 1])
                last.then_inc(S.cut.sem, 1)

            def scale(g, h):
                dve.wait_ge(S.factor.sem, S.factor.at(g, h + 1))
                if h == 0:
                    dve.wait_ge(S.keep.sem, S.keep.at(g))
                for it in range(T):
                    last = dve.tensor_scalar(S.cutp[:, h % 2, it, :], S.cutp[:, h % 2, it, :], S.fac[:, h, it:it + 1],
                                             S.kp[:, it:it + 1], ALU.mult, ALU.mult)
                last.then_inc(S.a.sem, 1)

            def maxima(g, h):
                dve.wait_ge(S.s_psum.sem, S.s_psum.at(g, h + 1))
                if h == 0:
                    if later(g):
                        dve.wait_ge(S.shift.sem, S.shift.all(g - 1))
                dve.reduce_max(S.mx[:, h, :], view(BB[h % 2]), AX_X).then_inc(S.max.sem, 1)

            def copy_t(g, h):
                if h % 2 == 1:
                    dve.wait_ge(S.a_t_psum.sem, S.a_t_psum.at(g, h + 1))
                    dve.tensor_copy(S.at[:, h % 4, :, :], view(BB[3])).then_inc(S.a_t_dve.sem, 1)

            def slot_b(stage, g):
                if stage == "b_project":
                    dve.wait_ge(S.m_psum.sem, S.m_psum.at(g))
                    for it in range(T):
                        last = dve.tensor_tensor(S.m[:, it, :], BB[1][:, it * DIM:(it + 1) * DIM], S.b_m[:, :], ALU.add)
                    last.then_inc(S.m_sb.sem, 1)
                    dve.wait_ge(S.m_sb.sem, S.m_sb.at(g))
                    dve.tensor_tensor(S.sq, S.m, S.m, ALU.mult).then_inc(S.square.sem, 1)
                    dve.wait_ge(S.square.sem, S.square.at(g))
                    dve.reduce_sum(S.ss[:, :], S.sq.rearrange("p t (h n) -> p (t h) n", n=DHS), AX_X)\
                        .then_inc(S.sumsq.sem, 1)
                    dve.wait_ge(S.inorm.sem, S.inorm.at(g))
                    dve.tensor_tensor(S.u.rearrange("p t (h n) -> p (t h) n", n=DHS),
                                      S.m.rearrange("p t (h n) -> p (t h) n", n=DHS),
                                      S.inv[:, :].rearrange("p (h a) -> p h a", a=1).broadcast_to([P, T * HS, DHS]),
                                      ALU.mult).then_inc(S.unit.sem, 1)
                    dve.wait_ge(S.sem_psum.sem, S.sem_psum.at(g))
                    for it in range(T):
                        last = dve.tensor_tensor(S.sem[:, it, :], BB[0][:, it * DIM:(it + 1) * DIM], S.b_s[:, :], ALU.add)
                    last.then_inc(S.sem_sb.sem, 1)
                elif stage.startswith("b_head"):
                    n = int(stage[7:])
                    if n == 0:
                        maxima(g, 0)
                        maxima(g, 1)
                        cut(g, 0)
                    else:
                        if n + 1 < HS:
                            maxima(g, n + 1)
                        if n < HS:
                            cut(g, n)
                        if n - 1 < HS:
                            copy_t(g, n - 1)
                elif stage.startswith("b_scale"):
                    scale(g, int(stage[8:]))
                elif stage == "b_out":
                    dve.wait_ge(S.y_psum.sem, S.y_psum.at(g))
                    if later(g):
                        dve.wait_ge(stored.sem, stored.all(g - 1))
                    dve.tensor_tensor(S.norm.r[:, :, :], view(BB[0]), x2[:, :, :], ALU.add).then_inc(S.norm.sum.sem, 1)
                    dve_norm_stats(dve, S.norm, g)
                elif stage == "b_norm_out":
                    dve_norm_out(dve, S.norm, g)
                elif stage == "d_qkv":
                    d_qkv(g)
                elif stage == "d_scores":
                    d_scores(g)
                elif stage == "d_norm":
                    d_normalise(g)
                elif stage == "d_probs_01":
                    d_probs(g, (0, 1))
                elif stage == "d_probs_23":
                    d_probs(g, (2, 3))
                elif stage == "d_values":
                    d_values(g)
                elif stage == "d_out":
                    d_finish(g)
                elif stage == "d_norm_out":
                    dve_norm_out(dve, D.norm, g)

            loop(dve, slot_a, slot_b)

        @block.gpsimd
        def _(pool):
            pool.memset(W.gcn, 0.0).then_inc(gcn_zero, 1)
            pool.memset(C.ident[:, :], 0.0).then_inc(const_ready, 1)
            pool.memset(C.minus_one[:, :], -1.0)
            pool.memset(C.minus_half[:, :], -0.5).then_inc(const_ready, 1)
            pool.memset(C.ones[:, :], 1.0).then_inc(const_ready, 1)
            pool.wait_ge(const_ready, 3)
            pool.affine_select(out=C.ident[:, :], in_=C.ident[:, :], compare_op=ALU.not_equal, fill=1.0, base=0,
                               pattern=[[-1, P]], channel_multiplier=1).then_inc(const_ready, 1)
            pool.wait_ge(const_ready, 4)
            pool.tensor_copy(C.ident_bf[:, :], C.ident[:, :]).then_inc(const_ready, 1)
            pool.wait_ge(w_loaded, 16 * n_loads)
            pool.wait_ge(w_sb, SETUP_COPIES)
            a_scores, a_finish = pool_attention(pool, A, C)
            d_scores, d_finish = pool_attention(pool, D, C)

            def g_wh(g, h):
                pool.wait_ge(G.wh_hi.sem, G.wh_hi.at(g, h + 1))
                pool.tensor_tensor(G.wh[h % 2][1], G.whf[:, h % 2, :, :], G.wh[h % 2][0].bitcast(F32),
                                   ALU.subtract).then_inc(G.wh_sb.sem, 1)

            def g_a(g, h):
                pool.wait_ge(G.a_hi.sem, G.a_hi.at(g, h + 1))
                pool.tensor_tensor(G.am[h % 2][1], G.th[:, h % 2, :, :], G.am[h % 2][0].bitcast(F32),
                                   ALU.subtract).then_inc(G.a.sem, 1)

            def slot_a(stage, g):
                if stage == "a_inputs":
                    pool.wait_ge(x_loaded.sem, x_loaded.all(g))
                    pool.wait_ge(adj_a_loaded.sem, adj_a_loaded.all(g))
                    pool_attention_mask(pool, A, g, adj_a)
                    if later(g):
                        pool.wait_ge(G.x_t_psum.sem, G.x_t_psum.all(g - 1))
                        pool.wait_ge(G.x_ha_done.sem, G.x_ha_done.all(g - 1))
                    pool_bias(pool, A, x_in)
                    if later(g):
                        pool.wait_ge(G.adj_psum.sem, G.adj_psum.all(g - 1))
                    apart(pool)
                    pool.tensor_copy(G.adj_bf[:, :, :], adj_a[:, :, :]).then_inc(G.adj_bf_ready.sem, 1)
                elif stage == "a_scores":
                    a_scores(g)
                elif stage == "a_sum":
                    a_finish(g)
                elif stage == "g_0":
                    g_wh(g, 0)
                elif stage in ("g_1", "g_2", "g_3"):
                    g_a(g, int(stage[2:]) - 1)
                    g_wh(g, int(stage[2:]))
                elif stage == "g_4":
                    g_a(g, 3)
                elif stage == "g_ha_1":
                    pool.wait_ge(G.ha_sb.sem, G.ha_sb.at(g))
                    pool.wait_ge(A.norm.out.sem, A.norm.out.at(g))
                    if later(g):
                        pool.wait_ge(G.norm.sum.sem, G.norm.sum.all(g - 1))
                    pool.tensor_tensor(G.x_ha[:, :, :], G.ha[:, :, :], x1[:, :, :], ALU.add).then_inc(G.x_ha_done.sem, 1)
                elif stage == "g_mix":
                    pool_norm(pool, G.norm, C, g)

            def shift(g, h):
                pool.wait_ge(S.max.sem, S.max.at(g, h + 1))
                if h == 0:
                    if later(g):
                        pool.wait_ge(S.exp.sem, S.exp.all(g - 1))
                apart(pool)
                pool.tensor_scalar(S.sh[:, h, :], S.mx[:, h, :], MAX_FLOOR, -(DHS ** -0.5), ALU.max, ALU.mult).then_inc(S.shift.sem, 1)

            def sum_drop(g, h):
                pool.wait_ge(S.exp.sem, S.exp.at(g, h + 1))
                pool.tensor_tensor(S.sd[:, h, :], S.sums[:, h, :], S.drop[:, :], ALU.add).then_inc(S.sum_drop.sem, 1)

            def factor(g, h):
                pool.wait_ge(S.sum_drop.sem, S.sum_drop.at(g, h + 1))
                pool.wait_ge(S.cut.sem, S.cut.at(g, h + 1))
                pool.tensor_tensor(S.den[:, h, :], S.dsum[:, h, :], S.sd[:, h, :], ALU.add).then_inc(S.denominator.sem, 1)
                pool.wait_ge(S.denominator.sem, S.denominator.at(g, h + 1))
                if h == 0:
                    if later(g):
                        pool.wait_ge(S.a.sem, S.a.all(g - 1))
                pool.tensor_tensor(S.fac[:, h, :], S.den[:, h, :], C.minus_one[:, 0:T], ALU.pow).then_inc(S.factor.sem, 1)

            def slot_b(stage, g):
                if stage == "b_x_t":
                    pool.wait_ge(adj_b_loaded.sem, adj_b_loaded.at(g, 16))
                    if later(g):
                        pool.wait_ge(S.s_psum.sem, S.s_psum.all(g - 1))
                    apart(pool)
                    pool.tensor_scalar(S.add[:, :, :], adj_b[:, :, :], MASKED, None, ALU.mult).then_inc(S.mask.sem, 1)
                    if later(g):
                        pool.wait_ge(S.a.sem, S.a.all(g - 1))
                        pool.wait_ge(S.sum_drop.sem, S.sum_drop.all(g - 1))
                    apart(pool)
                    pool.tensor_copy(S.drop[:, :], adj_b[:, :, 0])
                    pool.tensor_scalar(S.kp[:, :], adj_b[:, :, 0], -1.0, 1.0, ALU.mult, ALU.add).then_inc(S.keep.sem, 1)
                elif stage == "b_project":
                    pool.wait_ge(S.sumsq.sem, S.sumsq.at(g))
                    apart(pool)
                    pool.tensor_scalar(S.fl[:, :], S.ss[:, :], COS_EPS * COS_EPS, None, ALU.max).then_inc(S.floor.sem, 1)
                    pool.wait_ge(S.floor.sem, S.floor.at(g))
                    pool.tensor_tensor(S.inv[:, :], S.fl[:, :], C.minus_half[:, :], ALU.pow).then_inc(S.inorm.sem, 1)
                    pool.wait_ge(S.keep.sem, S.keep.at(g))
                elif stage.startswith("b_head"):
                    n = int(stage[7:])
                    if n == 0:
                        shift(g, 0)
                        shift(g, 1)
                        sum_drop(g, 0)
                        factor(g, 0)
                        sum_drop(g, 1)
                    elif n < HS:
                        if n + 1 < HS:
                            shift(g, n + 1)
                        factor(g, n)
                        if n + 1 < HS:
                            sum_drop(g, n + 1)
                elif stage == "b_out":
                    pool_norm(pool, S.norm, C, g)
                elif stage == "d_x_t":
                    pool_attention_mask(pool, D, g, adj_b)
                    pool.wait_ge(S.norm.out.sem, S.norm.out.at(g))
                    pool.wait_ge(D.x_t_psum.sem, D.x_t_psum.at(g))
                    pool_bias(pool, D, x3)
                elif stage == "d_scores":
                    d_scores(g)
                elif stage == "d_out":
                    d_finish(g)

            loop(pool, slot_a, slot_b)


INPUTS = ["x", "adj", "L0_gnn_Wq", "L0_gnn_Wk", "L0_gnn_Wv", "L0_gnn_Wo", "L0_gnn_bo", "L1_gnn_W", "L1_gnn_bW", "L1_gnn_attn",
          "L1_gnn_A_w", "L1_gnn_fc_w", "L1_gnn_g1_w", "L1_gnn_g2_w", "L1_gnn_gbias", "L2_gnn_map_w", "L2_gnn_map_b",
          "L2_gnn_q_w", "L2_gnn_q_b", "L2_gnn_k_w", "L2_gnn_k_b", "L2_gnn_gcn_map_w", "L2_gnn_gcn_map_b", "L2_gnn_gcn_W",
          "L3_gnn_Wq", "L3_gnn_Wk", "L3_gnn_Wv", "L3_gnn_Wo", "L3_gnn_bo"]


def kernel(**inputs):
    import concourse.bacc as bacc
    from concourse.bass_utils import run_bass_kernel_spmd

    nc = bacc.Bacc("TRN2", target_bir_lowering=False, num_devices=1)
    arrays, dram = {}, {}
    for name in INPUTS:
        a = np.ascontiguousarray(inputs[name])
        arrays[f"in_{name}"] = a
        dram[name] = nc.dram_tensor(f"in_{name}", a.shape, mybir.dt.from_np(a.dtype), kind="ExternalInput").ap()
    out = nc.dram_tensor("out", (GRAPHS, NODES, DIM), F32, kind="ExternalOutput").ap()
    build(nc, dram, out)
    result = run_bass_kernel_spmd(nc, [arrays], core_ids=[0])
    return result.results[0]["out"]
```
